# Optimizing a Trainium2 kernel written in Bass

```python
import numpy as np
import jax
import jax.numpy as jnp

def _softmax(x, axis=-1):
    return jax.nn.softmax(x, axis=axis)

def _gelu(x):
    return jax.nn.gelu(x, approximate=True)

def _silu(x):
    return jax.nn.silu(x)

def _sigmoid(x):
    return jax.nn.sigmoid(x)

def _layernorm(x, axis=-1, eps=1e-05):
    m = jnp.mean(x, axis=axis, keepdims=True)
    v = jnp.var(x, axis=axis, keepdims=True)
    return (x - m) / jnp.sqrt(v + eps)

def _scatter_add(tgt, idx, src, axis=0):
    return tgt.at[idx].add(src)

def _segment_sum(src, seg, n):
    return jax.ops.segment_sum(src, seg, n)
kernel_name = 'mk_decoder_postln_d1_seqx_r8_126d8b'

def setup_inputs(seed: int=0):
    np.random.seed(seed)
    _w = jnp.asarray

    def _rec_inputs():
        import jax
        import jax.numpy as jnp
        _rk = jax.random.key(seed)
        x = 7.22e-05 + 1 * jax.random.normal(jax.random.fold_in(_rk, 1), (4, 512, 128), jnp.float32)
        _lenS = 512 - jax.random.randint(jax.random.fold_in(_rk, 7), (4,), 0, max(1, 512 // 4) + 1, jnp.int32)
        _lenS2 = 154 - jax.random.randint(jax.random.fold_in(_rk, 8), (4,), 0, max(1, 154 // 4) + 1, jnp.int32)
        _ctx_768P = jax.random.normal(jax.random.fold_in(_rk, 11), (4, 16, 96), jnp.float32)
        _ctx_768c = jax.random.dirichlet(jax.random.fold_in(_rk, 511), 0.3 * jnp.ones((16,), jnp.float32), (4, 154))
        _ctx_768t = jnp.einsum('bsk,bkd->bsd', _ctx_768c, _ctx_768P)
        _ctx_768t = _ctx_768t * jax.lax.rsqrt(jnp.mean(jnp.square(_ctx_768t)) + 1e-12) * 0.953939
        ctx_768 = 2.09791e-05 + 1.00001 * (_ctx_768t + 0.3 * jax.random.normal(jax.random.fold_in(_rk, 611), (4, 154, 96), jnp.float32))
        return (x, ctx_768)
    x, ctx_768 = _rec_inputs()

    def _L0_attn_setup():
        import jax, jax.numpy as jnp
        import numpy as np
        BATCH, L, DM, N, R = (2, 256, 128, 16, 64)
        DT_MIN, DT_MAX = (0.001, 0.1)
        key = jax.random.key(seed)
        ks = jax.random.split(key, 6)
        x = jax.random.normal(ks[0], (BATCH, L, DM), jnp.float32)
        W_in = jax.random.normal(ks[1], (DM, 2 * N), jnp.float32) / np.sqrt(DM)
        b_in = jnp.zeros((2 * N,), jnp.float32)
        W_dt1 = jax.random.normal(ks[2], (DM, R), jnp.float32) / np.sqrt(DM)
        b_dt1 = jnp.zeros((R,), jnp.float32)
        dt_std = R ** (-0.5)
        W_dt2 = jax.random.uniform(ks[3], (R, DM), jnp.float32, minval=-dt_std, maxval=dt_std)
        u = jax.random.uniform(ks[4], (DM,), jnp.float32)
        dt0 = jnp.exp(u * (np.log(DT_MAX) - np.log(DT_MIN)) + np.log(DT_MIN))
        b_dt2 = dt0 + jnp.log(-jnp.expm1(-dt0))
        A_row = -(1.0 + jnp.arange(N, dtype=jnp.float32))
        A = jnp.tile(A_row[None, None, None, :], (1, 1, DM, 1))
        D = jnp.ones((DM,), jnp.float32)
        return {'x': x, 'W_in': W_in, 'b_in': b_in, 'W_dt1': W_dt1, 'b_dt1': b_dt1, 'W_dt2': W_dt2, 'b_dt2': b_dt2, 'A': A, 'D': D}
    _L0_attn_all = _L0_attn_setup()
    _L0_attn_in = {k: v for k, v in _L0_attn_all.items() if k in ('W_in', 'b_in', 'W_dt1', 'b_dt1', 'W_dt2', 'b_dt2', 'A', 'D')}
    del _L0_attn_all

    def _L0_xattn_setup():
        import jax, jax.numpy as jnp
        import numpy as np
        NUM_HEADS = 16
        key = jax.random.key(seed)
        ks = jax.random.split(key, 8)
        dim, cond_dim = (128, 96)
        B, N, condN = (4, 256, 128)
        s = lambda k, shp, fan: jax.random.normal(k, shp, dtype=jnp.float32) * fan ** (-0.5)
        return {'x': jax.random.normal(ks[0], (B, N, dim), dtype=jnp.float32), 'cond': jax.random.normal(ks[1], (B, condN, cond_dim), dtype=jnp.float32), 'q_w': s(ks[2], (dim, dim), dim), 'q_b': jnp.zeros((dim,), jnp.float32), 'kv_w': s(ks[3], (cond_dim, 2 * dim), cond_dim), 'kv_b': jnp.zeros((2 * dim,), jnp.float32), 'proj_w': s(ks[4], (dim, dim), dim), 'proj_b': jnp.zeros((dim,), jnp.float32)}
    _L0_xattn_all = _L0_xattn_setup()
    _L0_xattn_in = {k: v for k, v in _L0_xattn_all.items() if k in ('q_w', 'q_b', 'kv_w', 'kv_b', 'proj_w', 'proj_b')}
    del _L0_xattn_all

    def _L0_ffn_setup():
        import jax, jax.numpy as jnp
        import numpy as np
        D, H, E, K = (128, 128, 8, 2)

        def _moe(x, router_w, w_in, b_in, w_out, b_out):
            B, S, Dm = x.shape
            T = B * S
            x2 = x.reshape(T, Dm)
            logits = x2 @ router_w
            probs = jax.nn.softmax(logits, axis=-1)
            top_p, top_e = jax.lax.top_k(probs, K)
            flat_e = top_e.reshape(-1)
            flat_p = top_p.reshape(-1)
            tok = jnp.repeat(jnp.arange(T), K)
            order = jnp.argsort(flat_e)
            se, sp, st = (flat_e[order], flat_p[order], tok[order])
            xd = x2[st]
            N = xd.shape[0]
            h = jnp.zeros((N, H), x.dtype)
            for e in range(E):
                m = (se == e)[:, None]
                h = h + jnp.where(m, jax.nn.gelu(xd @ w_in[e] + b_in[e]), 0.0)
            y = jnp.zeros((N, Dm), x.dtype)
            for e in range(E):
                m = (se == e)[:, None]
                y = y + jnp.where(m, h @ w_out[e] + b_out[e], 0.0)
            y = y * sp[:, None]
            out = jnp.zeros((T, Dm), x.dtype).at[st].add(y)
            return out.reshape(B, S, Dm)
        key = jax.random.key(seed)
        ks = jax.random.split(key, 5)
        s = lambda k, shape, scale: jax.random.normal(k, shape, dtype=jnp.float32) * scale
        return {'input_batch': s(ks[0], (2, 64, D), 1.0), 'router_w': s(ks[1], (D, E), D ** (-0.5)), 'w_in': s(ks[2], (E, D, H), D ** (-0.5)), 'b_in': jnp.zeros((E, H), jnp.float32), 'w_out': s(ks[3], (E, H, D), H ** (-0.5)), 'b_out': jnp.zeros((E, D), jnp.float32)}
    _L0_ffn_all = _L0_ffn_setup()
    _L0_ffn_in = {k: v for k, v in _L0_ffn_all.items() if k in ('router_w', 'w_in', 'b_in', 'w_out', 'b_out')}
    del _L0_ffn_all
    return {'x': x, 'ctx_768': ctx_768, 'L0_attn_W_in': _L0_attn_in['W_in'], 'L0_attn_b_in': _L0_attn_in['b_in'], 'L0_attn_W_dt1': _L0_attn_in['W_dt1'], 'L0_attn_b_dt1': _L0_attn_in['b_dt1'], 'L0_attn_W_dt2': _L0_attn_in['W_dt2'], 'L0_attn_b_dt2': _L0_attn_in['b_dt2'], 'L0_attn_A': _L0_attn_in['A'], 'L0_attn_D': _L0_attn_in['D'], 'L0_xattn_q_w': _L0_xattn_in['q_w'], 'L0_xattn_q_b': _L0_xattn_in['q_b'], 'L0_xattn_kv_w': _L0_xattn_in['kv_w'], 'L0_xattn_kv_b': _L0_xattn_in['kv_b'], 'L0_xattn_proj_w': _L0_xattn_in['proj_w'], 'L0_xattn_proj_b': _L0_xattn_in['proj_b'], 'L0_ffn_router_w': _L0_ffn_in['router_w'], 'L0_ffn_w_in': _L0_ffn_in['w_in'], 'L0_ffn_b_in': _L0_ffn_in['b_in'], 'L0_ffn_w_out': _L0_ffn_in['w_out'], 'L0_ffn_b_out': _L0_ffn_in['b_out']}

def reference(x, ctx_768, L0_attn_W_in, L0_attn_b_in, L0_attn_W_dt1, L0_attn_b_dt1, L0_attn_W_dt2, L0_attn_b_dt2, L0_attn_A, L0_attn_D, L0_xattn_q_w, L0_xattn_q_b, L0_xattn_kv_w, L0_xattn_kv_b, L0_xattn_proj_w, L0_xattn_proj_b, L0_ffn_router_w, L0_ffn_w_in, L0_ffn_b_in, L0_ffn_w_out, L0_ffn_b_out):
    import jax
    import jax.numpy as jnp

    def _L0_attn_ref(x, W_in, b_in, W_dt1, b_dt1, W_dt2, b_dt2, A, D):
        import jax, jax.numpy as jnp
        import numpy as np
        BATCH, L, DM, N, R = (2, 256, 128, 16, 64)
        DT_MIN, DT_MAX = (0.001, 0.1)
        BC = x @ W_in + b_in
        Bm, Cm = (BC[..., :N], BC[..., N:])
        dt = jax.nn.softplus((x @ W_dt1 + b_dt1) @ W_dt2 + b_dt2)
        dt = jnp.clip(dt, 1e-07, 1000000.0)
        tmp = A * dt[..., None]
        A_bar = jnp.exp(tmp)
        B_barX = jnp.expm1(tmp) / tmp * dt[..., None] * Bm[:, :, None, :] * x[..., None]

        def combine(e1, e2):
            a1, b1 = e1
            a2, b2 = e2
            return (a1 * a2, a2 * b1 + b2)
        _, h = jax.lax.associative_scan(combine, (A_bar, B_barX), axis=1)
        return jnp.sum(h * Cm[:, :, None, :], axis=-1) + D * x

    def _L0_xattn_ref(x, cond, q_w, q_b, kv_w, kv_b, proj_w, proj_b):
        import jax, jax.numpy as jnp
        import numpy as np
        NUM_HEADS = 16
        B, N, C = x.shape
        condN = cond.shape[1]
        H = NUM_HEADS
        hd = C // H
        scale = hd ** (-0.5)
        q = (x @ q_w + q_b).reshape(B, N, H, hd).transpose(0, 2, 1, 3)
        kv = (cond @ kv_w + kv_b).reshape(B, condN, 2, H, hd)
        k = kv[:, :, 0].transpose(0, 2, 1, 3)
        v = kv[:, :, 1].transpose(0, 2, 1, 3)
        attn = jnp.einsum('bhnd,bhmd->bhnm', q * scale, k)
        attn = jax.nn.softmax(attn, axis=-1)
        out = jnp.einsum('bhnm,bhmd->bhnd', attn, v)
        out = out.transpose(0, 2, 1, 3).reshape(B, N, C)
        return out @ proj_w + proj_b

    def _L0_ffn_ref(input_batch, router_w, w_in, b_in, w_out, b_out):
        import jax, jax.numpy as jnp
        import numpy as np
        D, H, E, K = (128, 128, 8, 2)

        def _moe(x, router_w, w_in, b_in, w_out, b_out):
            B, S, Dm = x.shape
            T = B * S
            x2 = x.reshape(T, Dm)
            logits = x2 @ router_w
            probs = jax.nn.softmax(logits, axis=-1)
            top_p, top_e = jax.lax.top_k(probs, K)
            flat_e = top_e.reshape(-1)
            flat_p = top_p.reshape(-1)
            tok = jnp.repeat(jnp.arange(T), K)
            order = jnp.argsort(flat_e)
            se, sp, st = (flat_e[order], flat_p[order], tok[order])
            xd = x2[st]
            N = xd.shape[0]
            h = jnp.zeros((N, H), x.dtype)
            for e in range(E):
                m = (se == e)[:, None]
                h = h + jnp.where(m, jax.nn.gelu(xd @ w_in[e] + b_in[e]), 0.0)
            y = jnp.zeros((N, Dm), x.dtype)
            for e in range(E):
                m = (se == e)[:, None]
                y = y + jnp.where(m, h @ w_out[e] + b_out[e], 0.0)
            y = y * sp[:, None]
            out = jnp.zeros((T, Dm), x.dtype).at[st].add(y)
            return out.reshape(B, S, Dm)
        return _moe(input_batch, router_w, w_in, b_in, w_out, b_out)
    x = _layernorm(x + _L0_attn_ref(x, L0_attn_W_in, L0_attn_b_in, L0_attn_W_dt1, L0_attn_b_dt1, L0_attn_W_dt2, L0_attn_b_dt2, L0_attn_A, L0_attn_D), axis=-1)
    x = _layernorm(x + _L0_xattn_ref(x, ctx_768, L0_xattn_q_w, L0_xattn_q_b, L0_xattn_kv_w, L0_xattn_kv_b, L0_xattn_proj_w, L0_xattn_proj_b), axis=-1)
    x = _layernorm(x + _L0_ffn_ref(x, L0_ffn_router_w, L0_ffn_w_in, L0_ffn_b_in, L0_ffn_w_out, L0_ffn_b_out), axis=-1)
    return x

_drawn_inputs = setup_inputs


def setup_inputs(seed=0):
    import zlib

    import numpy as np

    out = dict(_drawn_inputs(seed))
    spreads = {'L0_attn_b_in': (0.0, 0.4),
     'L0_attn_b_dt1': (0.0, 0.8),
     'L0_attn_D': (1.0, 0.2),
     'L0_xattn_q_b': (0.0, 0.277),
     'L0_xattn_kv_b': (0.0, 0.1),
     'L0_xattn_proj_b': (0.0, 0.1),
     'L0_ffn_b_in': (0.0, 0.283),
     'L0_ffn_b_out': (0.0, 0.1)}
    factors = {}
    for name, (base, spread) in spreads.items():
        noise = np.random.default_rng([zlib.crc32(name.encode()), seed]).standard_normal(out[name].shape)
        drawn = base * np.exp(spread * noise) if base else spread * noise
        out[name] = jnp.asarray(drawn.astype(out[name].dtype))
    for name, factor in factors.items():
        out[name] = (out[name] * factor).astype(out[name].dtype)
    return out
```

```python
import concourse.bass as bass
from concourse import mybir
from contextlib import ExitStack

B, L, D, N, R = 4, 512, 128, 16, 64
HEADS, HD = 16, 8
MC, DC = 154, 96
MREM = MC - 128
MPAD = 32
E, NT = 8, L // 128
DT_MIN, DT_MAX, EPS = 1e-7, 1e6, 1e-5
SCALE = float(HD) ** -0.5
MAXROW = 96
KS = MAXROW + 3


def pack_layout():
    widths = [("w_in3", 96), ("w_dt1", R), ("w_dt2", D), ("A", N), ("D", 1), ("b_dt2", 1), ("b_dt1", 1),
              ("b_in3", 1), ("eye3", 32), ("ident", 128), ("iota", NT * E),
              ("q_w", D), ("q_b", 1), ("k_w", D), ("k_b", 1), ("v_w", D), ("v_b", D), ("p_w", D), ("p_b", 1),
              ("r_w", E), ("e_bin", E), ("e_bout", D), ("e_win", E * D), ("e_wout", E * D)]
    at, out = 0, {}
    for name, w in widths:
        out[name] = (at, w)
        at += w
    return out, at


ST_ITEMS = [(r, s) for r in range(4) for s in range(5)]


def step_order():
    s1 = [[("x", 0), ("dt1", 0), ("dt2", 0), ("bc", 0)]]
    for n in range(N):
        s1.append([("ae", n), ("sc", n)])
    pre = [[("cx", 0), ("ln", 0)], [("kv", 0)], [("q", 0)]]
    pre += [[("mx", g) for g in range(6 * c, 6 * c + 6)] for c in range(NT)]
    pre += [[("mt", 0)]]
    heads = []
    for j in range(20):
        heads.append([("hd", j)] + ([("pv", j - 1)] if j % 10 else []) + ([("pv", j), ("on", j // 10)] if j % 10 == 9 else []))
    post = [[("pj", 0)], [("ln", 1)], [("ro", 0)]]
    experts = [[("ex", e)] for e in range(E)]
    last = [[("ln", 2)]]
    s23 = pre + heads + post + experts + last
    order, i = list(s1[0]), 0
    slots = s1[1:]
    per = len(s23) / len(slots)
    exps = [t for s in slots for t in s if t[0] == "ae"]
    sent = 0
    for n in range(N):
        upto = round((n + 1) * per)
        want = min(N, n + 4 + (n >= 8) * 8)
        while sent < want:
            order.append(exps[sent])
            sent += 1
        order.append(("sc", n))
        while i < upto and i < len(s23):
            order += s23[i]
            i += 1
    order.append(("s1", 0))
    return order


ORDER = step_order()
S1_TASKS = {"x", "dt1", "dt2", "bc", "ae", "sc", "s1"}


def decoder_block(nc, xT, ctxT, wpack, out):
    F32, BF16, U32 = mybir.dt.float32, mybir.dt.bfloat16, mybir.dt.uint32
    ALU, ACT, AX = mybir.AluOpType, mybir.ActivationFunctionType, mybir.AxisListType
    cols, WC = pack_layout()
    ctx = ExitStack()
    with ctx:
        def sb(name, shape, dt=F32):
            return ctx.enter_context(nc.sbuf_tensor(name, shape, dt))

        def sem(name):
            return ctx.enter_context(nc.semaphore(name))

        W = sb("W", [128, WC])
        xall = sb("xall", [128, B, L])
        call = sb("call", [DC, B, MC])
        consts = sb("consts", [128, 2])
        sel = sb("sel", [96, 32, 128], BF16)
        mean_w = sb("mean_w", [128, 128])
        onepD = sb("onepD", [128, 1])
        rA = sb("rA", [128, N])
        xcur = sb("xcur", [128, L])
        z1 = sb("z1", [R, L])
        z = sb("z", [128, L])
        zabs = sb("zabs", [128, L])
        zexp = sb("zexp", [128, L])
        zlog = sb("zlog", [128, L])
        dtr = sb("dtr", [128, L])
        dt = sb("dt", [128, L])
        bcf = sb("bcf", [96, L])
        bcr = sb("bcr", [96, L])
        bct = sb("bct", [96, L], BF16)
        bcs = sb("bcs", [96, L], BF16)
        abar = sb("abar", [128, N, L])
        ub = sb("ub", [128, L])
        bbar = sb("bbar", [128, L])
        hst = sb("hst", [128, L])
        hc = sb("hc", [128, 4, L])
        hpair = sb("hpair", [128, 2, L])
        s1 = sb("s1", [128, L])
        lnin = [s1, sb("s2", [128, L]), sb("s3", [128, L])]
        lnout = [sb("x1", [128, L]), sb("x2", [128, L]), sb("x3", [128, L])]
        xc = sb("xc", [128, L])
        sq = sb("sq", [128, L])
        lnv = sb("lnv", [128, L])
        rstd = sb("rstd", [128, L])
        ccur = sb("ccur", [DC, MC])
        kf = sb("kf", [128, MC])
        kr = sb("kr", [128, MC])
        kp = [sb(f"kp{j}", [128, 128 + MPAD], BF16) for j in range(3)]
        qf = sb("qf", [128, L])
        qr = sb("qr", [128, L])
        qp = [sb(f"qp{j}", [128, L], BF16) for j in range(3)]
        ks = sb("ks", [KS, HEADS, 128 + MPAD], BF16)
        qs = sb("qs", [KS, HEADS, L], BF16)
        vp = sb("vp", [128, HEADS * 128 + 64])
        vr = sb("vr", [128, 4 * 128 + 64])
        mx = sb("mx", [128, NT, HEADS])
        nmf = sb("nmf", [HEADS, L])
        nmr = sb("nmr", [HEADS, L])
        nmp = [sb(f"nmp{j}", [HEADS, L], BF16) for j in range(3)]
        pt = sb("pt", [128, 3, L])
        rden = sb("rden", [64, 2, L])
        oT = sb("oT", [128, L])
        lmx = sb("lmx", [128, NT])
        lg = sb("lg", [128, NT, E])
        pe_ = sb("pe_", [128, NT, E])
        psm = sb("psm", [128, NT])
        prs = sb("prs", [128, NT])
        m8 = sb("m8", [128, NT, 8])
        ix = sb("ix", [128, NT, 8], U32)
        ixf = sb("ixf", [128, NT, 8])
        mk = sb("mk", [128, 2, NT, E])
        mks = sb("mks", [128, NT, E])
        wgt = sb("wgt", [128, NT, E])
        wgn = sb("wgn", [128, NT, E])
        wT = sb("wT", [E, L])
        wr = sb("wr", [E, L])
        wr2 = sb("wr2", [E, L], BF16)
        ws = sb("ws", [96, L], BF16)
        gl = sb("gl", [128, 2, L])
        gw = sb("gw", [128, 2, L])

        def ps(name):
            return ctx.enter_context(nc.psum_tensor(name, [128, 512], F32))

        psB, psC, psY, psS0, psS1, psO0, psO1, psM = [ps(n) for n in ("psB", "psC", "psY", "psS0", "psS1", "psO0", "psO1", "psM")]
        psS, psO = [psS0, psS1], [psO0, psO1]

        def w(name, rows=128, at=0, n=None):
            first, width = cols[name]
            return W[0:rows, first + at:first + at + (width if n is None else n)]

        ident = w("ident")

        loaded, consts_set, zeroed, ones_set = sem("loaded"), sem("consts_set"), sem("zeroed"), sem("ones_set")
        inv_done = sem("inv_done")
        x_copied = sem("x_copied")
        z1_mm, z1_done = sem("z1_mm"), sem("z1_done")
        z2_mm, z_done, zabs_done, zexp_done, zlog_done = [sem(n) for n in ("z2_mm", "z_done", "zabs_done", "zexp_done", "zlog_done")]
        dtr_done, dt_done = sem("dtr_done"), sem("dt_done")
        bc_mm, bcf_done, bc_first, bcr_done, bc_second, bcs_done = [
            sem(n) for n in ("bc_mm", "bcf_done", "bc_first", "bcr_done", "bc_second", "bcs_done")]
        b_bcast, c_bcast = sem("b_bcast"), sem("c_bcast")
        a_done, u_done, bb_done, h_done, hc_done = [sem(n) for n in ("a_done", "u_done", "bb_done", "h_done", "hc_done")]
        pair_done, y_mm, s1_done = sem("pair_done"), sem("y_mm"), sem("s1_done")
        mean_mm, xc_done, sq_done, var_mm, lnv_done, rstd_done, ln_done = [
            sem(n) for n in ("mean_mm", "xc_done", "sq_done", "var_mm", "lnv_done", "rstd_done", "ln_done")]
        c_copied, k_mm, v_mm, kf_done, kr_done, k_stacked, v_done = [
            sem(n) for n in ("c_copied", "k_mm", "v_mm", "kf_done", "kr_done", "k_stacked", "v_done")]
        q_mm, qf_done, qr_done, q_stacked = [sem(n) for n in ("q_mm", "qf_done", "qr_done", "q_stacked")]
        sc_mm, mx_done, mt_mm, nmf_done, nmr_done, nm_stacked = [
            sem(n) for n in ("sc_mm", "mx_done", "mt_mm", "nmf_done", "nmr_done", "nm_stacked")]
        k_part, q_part, nm_part = [[sem(f"{n}_part{j}") for j in range(3)] for n in ("k", "q", "nm")]
        st_mm, p_done, pv_mm, rden_done, o_done, pj_mm, s2_done = [
            sem(n) for n in ("st_mm", "p_done", "pv_mm", "rden_done", "o_done", "pj_mm", "s2_done")]
        r_mm, r_step, re_done, wt_mm, ws_done = [sem(n) for n in ("r_mm", "r_step", "re_done", "wt_mm", "ws_done")]
        up_mm, wb_mm, g_done, gw_done, dn_mm, s3_done, stored = [
            sem(n) for n in ("up_mm", "wb_mm", "g_done", "gw_done", "dn_mm", "s3_done", "stored")]

        K_DMAS, NM_DMAS = 9 * 16, 3 * 16

        def nth(batch, per_batch, i):
            return batch * per_batch + i + 1

        def tasks(p, b):
            return [(t, i) for t, i in ORDER if (p is not None if t in S1_TASKS else b is not None)]

        def run_steps(step, engine_fori):
            step(0, None)
            with engine_fori(0, B - 1) as b:
                step(b + 1, b)
            step(None, B - 1)

        block = ctx.enter_context(nc.Block())

        @block.sync
        def _(sp):
            first = cols["q_w"][0]
            sp.dma_start(W[:, 0:first], wpack[:, 0:first]).then_inc(loaded, 16)
            sp.dma_start(xall[:, 0, :], xT[:, 0, :]).then_inc(loaded, 16)
            sp.dma_start(call[:, :, :], ctxT).then_inc(loaded, 16)
            sp.dma_start(xall[:, 1:B, :], xT[:, 1:B, :]).then_inc(loaded, 16)
            sp.dma_start(W[:, first:WC], wpack[:, first:WC]).then_inc(loaded, 16)

            sp.wait_ge(ones_set, 21)

            def step(p, b):
                for t, i in tasks(p, b):
                    if t == "kv":
                        for j in range(3):
                            sp.wait_ge(k_part[j], nth(b, 1, 0))
                            for i_ in range(3):
                                row = (i_ * 3 + j) * HD
                                sp.dma_start(ks[row:row + HD, :, :], kp[j][:, :]).then_inc(k_stacked, 16)
                    elif t == "q":
                        for i_ in range(3):
                            sp.wait_ge(q_part[i_], nth(b, 1, 0))
                            for j in range(3):
                                row = (i_ * 3 + j) * HD
                                sp.dma_start(qs[row:row + HD, :, :], qp[i_][:, :]).then_inc(q_stacked, 16)
                    elif t == "mt":
                        for j in range(3):
                            sp.wait_ge(nm_part[j], nth(b, 1, 0))
                            sp.dma_start(qs[MAXROW + j:MAXROW + j + 1, :, :], nmp[j][:, :]).then_inc(nm_stacked, 16)
                    elif t == "ln" and i == 2:
                        sp.wait_ge(ln_done, nth(b, 3, 2))
                        sp.dma_start(out[bass.ds(b, 1), :, :], lnout[2][:, :]).then_inc(stored, 16)

            run_steps(step, sp.Fori)
            sp.wait_ge(stored, 16 * B)

        @block.gpsimd
        def _(pool):
            pool.memset(consts[:, 0:1], EPS).then_inc(consts_set, 1)
            pool.memset(consts[:, 1:2], 1.0).then_inc(consts_set, 1)
            pool.memset(mean_w[:, :], 1.0 / D).then_inc(consts_set, 1)
            pool.wait_ge(loaded, 16 * 5)
            pool.tensor_copy(sel[:, :, :], w("eye3", 96).unsqueeze(2).to_broadcast([96, 32, 128])).then_inc(consts_set, 1)
            pool.memset(qs[:, :, :], 0.0).then_inc(zeroed, 1)
            pool.memset(ks[:, :, :], 0.0).then_inc(zeroed, 1)
            pool.memset(vp[:, :], 0.0).then_inc(zeroed, 1)
            pool.memset(vr[:, :], 0.0).then_inc(zeroed, 1)
            pool.memset(ws[:, :], 0.0).then_inc(zeroed, 1)
            for j in range(3):
                pool.memset(kp[j][:, :], 0.0).then_inc(zeroed, 1)

            def ones_columns(tile, rows, first, n):
                v = tile[rows[0]:rows[1], first:first + n * 136].rearrange("p (i c) -> p i c", c=136)[:, :, 0:HD]
                return v

            pool.wait_ge(zeroed, 8)
            pool.memset(ks[MAXROW:KS, :, 0:MC], 1.0).then_inc(ones_set, 1)
            pool.wait_ge(ones_set, 1)
            for g in range(2):
                pool.memset(ones_columns(vp, (0, 128), g * 1024 + 64, 7), 1.0).then_inc(ones_set, 1)
                pool.memset(vp[:, g * 1024 + 7 * 136 + 64:g * 1024 + 7 * 136 + 64 + HD], 1.0).then_inc(ones_set, 1)
            for j in range(4):
                for r in range(4):
                    pool.wait_ge(ones_set, 5 + 4 * j + r)
                    c = r * 128 + (r % 2) * 32 + j * HD + 64
                    pool.memset(vr[32 * j:32 * j + MREM, c:c + HD], 1.0).then_inc(ones_set, 1)

            pool.wait_ge(ones_set, 21)

            def remainders(whole, rest, parts, first_copied, second_copied, rest_done, third_done, batch):
                pool.wait_ge(first_copied, nth(batch, 1, 0))
                pool.tensor_tensor(rest, whole, parts[0], ALU.subtract).then_inc(rest_done, 1)
                pool.wait_ge(second_copied, nth(batch, 1, 0))
                pool.tensor_tensor(parts[2], rest, parts[1], ALU.subtract).then_inc(third_done, 1)

            def step(p, b):
                for t, i in tasks(p, b):
                    if t == "x":
                        if b is not None:
                            pool.wait_ge(s1_done, p)
                        pool.tensor_copy(xcur[:, :], xall[:, bass.ds(p, 1), :]).then_inc(x_copied, 1)
                    elif t == "bc":
                        pool.wait_ge(bc_first, nth(p, 1, 0))
                        pool.tensor_tensor(bcr[:, :], bcf[:, :], bcs[:, :], ALU.subtract).then_inc(bcr_done, 1)
                    elif t == "sc" and i % 2:
                        k = i // 2
                        pool.wait_ge(hc_done, nth(p, N, i))
                        if k >= 2 or b is not None:
                            pool.wait_ge(y_mm, p * 8 + k - 1)
                        pool.tensor_tensor(hpair[:, k % 2, :], hc[:, (i - 1) % 4, :], hc[:, i % 4, :], ALU.add).then_inc(pair_done, 1)
                    elif t == "cx":
                        pool.wait_ge(v_mm, b * 5)
                        pool.tensor_copy(ccur[:, :], call[:, bass.ds(b, 1), :]).then_inc(c_copied, 1)
                    elif t == "kv":
                        pool.wait_ge(k_stacked, b * K_DMAS)
                        remainders(kf[:, :], kr[:, :], [kp[j][:, 0:MC] for j in range(3)],
                                   k_part[0], k_part[1], kr_done, k_part[2], b)
                    elif t == "q":
                        pool.wait_ge(q_stacked, b * K_DMAS)
                        remainders(qf[:, :], qr[:, :], [qp[j][:, :] for j in range(3)],
                                   q_part[0], q_part[1], qr_done, q_part[2], b)
                    elif t == "mt":
                        pool.wait_ge(nm_stacked, b * NM_DMAS)
                        remainders(nmf[:, :], nmr[:, :], [nmp[j][:, :] for j in range(3)],
                                   nm_part[0], nm_part[1], nmr_done, nm_part[2], b)

            run_steps(step, pool.Fori)

        @block.scalar
        def _(act):
            act.wait_ge(consts_set, 4)
            act.wait_ge(loaded, 16 * 5)
            act.wait_ge(zeroed, 8)
            eps, one = consts[:, 0:1], consts[:, 1:2]

            def roundings(whole, rest, parts, whole_done, rest_done, part_done, out_dmas, n_dmas, batch):
                act.wait_ge(out_dmas, batch * n_dmas)
                act.wait_ge(whole_done, nth(batch, 1, 0))
                nc.scalar.copy(parts[0], whole).then_inc(part_done[0], 1)
                act.wait_ge(rest_done, nth(batch, 1, 0))
                nc.scalar.copy(parts[1], rest).then_inc(part_done[1], 1)

            def step(p, b):
                for t, i in tasks(p, b):
                    if t == "dt1":
                        act.wait_ge(z1_mm, nth(p, 1, 0))
                        nc.scalar.activation(z1[:, :], psM[0:R, :], ACT.Identity, bias=w("b_dt1", R)).then_inc(z1_done, 1)
                    elif t == "dt2":
                        act.wait_ge(z2_mm, nth(p, 1, 0))
                        nc.scalar.activation(z[:, :], psM[:, :], ACT.Identity, bias=w("b_dt2")).then_inc(z_done, 1)
                        act.wait_ge(z_done, nth(p, 1, 0))
                        nc.scalar.activation(zabs[:, :], z[:, :], ACT.Abs).then_inc(zabs_done, 1)
                        act.wait_ge(zabs_done, nth(p, 1, 0))
                        nc.scalar.activation(zexp[:, :], zabs[:, :], ACT.Exp, scale=-1.0).then_inc(zexp_done, 1)
                        act.wait_ge(zexp_done, nth(p, 1, 0))
                        nc.scalar.activation(zlog[:, :], zexp[:, :], ACT.Ln, bias=one).then_inc(zlog_done, 1)
                    elif t == "bc":
                        act.wait_ge(bc_mm, nth(p, 1, 0))
                        nc.scalar.activation(bcf[:, :], psM[0:96, :], ACT.Identity, bias=w("b_in3", 96)).then_inc(bcf_done, 1)
                        act.wait_ge(bcf_done, nth(p, 1, 0))
                        nc.scalar.copy(bcs[:, :], bcf[:, :]).then_inc(bc_first, 1)
                        act.wait_ge(bcr_done, nth(p, 1, 0))
                        nc.scalar.copy(bct[64:96, :], bcr[64:96, :])
                        nc.scalar.copy(bcs[32:64, :], bcr[32:64, :]).then_inc(bc_second, 1)
                    elif t == "kv":
                        roundings(kf[:, :], kr[:, :], [kp[j][:, 0:MC] for j in range(2)],
                                  kf_done, kr_done, k_part, k_stacked, K_DMAS, b)
                    elif t == "q":
                        roundings(qf[:, :], qr[:, :], [qp[j][:, :] for j in range(2)],
                                  qf_done, qr_done, q_part, q_stacked, K_DMAS, b)
                    elif t == "mt":
                        roundings(nmf[:, :], nmr[:, :], [nmp[j][:, :] for j in range(2)],
                                  nmf_done, nmr_done, nm_part, nm_stacked, NM_DMAS, b)
                    elif t == "ae":
                        if i == 0:
                            act.wait_ge(dt_done, nth(p, 1, 0))
                        if b is not None:
                            act.wait_ge(h_done, nth(b, N, i))
                        nc.scalar.activation(abar[:, i, :], dt[:, :], ACT.Exp, scale=w("A", at=i, n=1)).then_inc(a_done, 1)
                    elif t == "ln":
                        act.wait_ge(xc_done, nth(b, 3, i))
                        nc.scalar.activation(sq[:, :], xc[:, :], ACT.Square).then_inc(sq_done, 1)
                        act.wait_ge(var_mm, nth(b, 3, i))
                        nc.scalar.activation(lnv[:, :], psM[:, :], ACT.Ln, bias=eps).then_inc(lnv_done, 1)
                        act.wait_ge(lnv_done, nth(b, 3, i))
                        nc.scalar.activation(rstd[:, :], lnv[:, :], ACT.Exp, scale=-0.5).then_inc(rstd_done, 1)
                    elif t == "hd":
                        act.wait_ge(st_mm, nth(b, 20, i))
                        if i >= 3:
                            act.wait_ge(pv_mm, nth(b, 20, i - 3))
                        nc.scalar.activation(pt[:, i % 3, :], psS[i % 2][:, :], ACT.Exp).then_inc(p_done, 1)
                    elif t == "ro":
                        act.wait_ge(r_step, nth(b, 13, 1))
                        nc.scalar.activation(pe_[:, :, :], lg[:, :, :], ACT.Exp).then_inc(re_done, 1)
                    elif t == "ex":
                        act.wait_ge(up_mm, nth(b, E, i))
                        if i >= 2:
                            act.wait_ge(gw_done, nth(b, E, i - 2))
                        nc.scalar.activation(gl[:, i % 2, :], psS[i % 2][:, :], ACT.Gelu_apprx_tanh,
                                             bias=w("e_bin", at=i, n=1)).then_inc(g_done, 1)

            run_steps(step, act.Fori)

        @block.vector
        def _(dve):
            dve.wait_ge(loaded, 16 * 5)
            nc.vector.reciprocal(rA[:, :], w("A")).then_inc(inv_done, 1)
            nc.vector.tensor_scalar(onepD[:, :], w("D"), 1.0, None, ALU.add).then_inc(inv_done, 1)
            dve.wait_ge(inv_done, 2)

            def per_tile(ap):
                return ap.unsqueeze(2).to_broadcast([128, NT, E])

            def step(p, b):
                for t, i in tasks(p, b):
                    if t == "dt2":
                        dve.wait_ge(zlog_done, nth(p, 1, 0))
                        nc.vector.scalar_tensor_tensor(out=dtr[:, :], in0=z[:, :], scalar=0.0, in1=zlog[:, :],
                                                       op0=ALU.max, op1=ALU.add).then_inc(dtr_done, 1)
                        dve.wait_ge(dtr_done, nth(p, 1, 0))
                        if b is not None:
                            dve.wait_ge(a_done, N * p)
                        nc.vector.tensor_scalar(dt[:, :], dtr[:, :], DT_MIN, DT_MAX, ALU.max, ALU.min).then_inc(dt_done, 1)
                    elif t == "bc":
                        dve.wait_ge(bc_second, nth(p, 1, 0))
                        nc.vector.tensor_tensor(bcs[64:96, :], bcr[64:96, :], bct[64:96, :], ALU.subtract).then_inc(bcs_done, 1)
                    elif t == "sc":
                        if i == 0:
                            dve.wait_ge(x_copied, nth(p, 1, 0))
                        dve.wait_ge(b_bcast, nth(p, N, i))
                        nc.vector.tensor_tensor(ub[:, :], psB[:, :], xcur[:, :], ALU.mult).then_inc(u_done, 1)
                        dve.wait_ge(u_done, nth(p, N, i))
                        dve.wait_ge(a_done, nth(p, N, i))
                        nc.vector.scalar_tensor_tensor(out=bbar[:, :], in0=abar[:, i, :], scalar=-1.0, in1=ub[:, :],
                                                       op0=ALU.add, op1=ALU.mult).then_inc(bb_done, 1)
                        dve.wait_ge(bb_done, nth(p, N, i))
                        nc.vector.tensor_tensor_scan(hst[:, :], abar[:, i, :], bbar[:, :], 0.0,
                                                     ALU.mult, ALU.add).then_inc(h_done, 1)
                        dve.wait_ge(h_done, nth(p, N, i))
                        dve.wait_ge(c_bcast, nth(p, N, i))
                        if i >= 4 or b is not None:
                            dve.wait_ge(pair_done, p * 8 + i // 2 - 1)
                        nc.vector.scalar_tensor_tensor(out=hc[:, i % 4, :], in0=hst[:, :], scalar=rA[:, i:i + 1], in1=psC[:, :],
                                                       op0=ALU.mult, op1=ALU.mult).then_inc(hc_done, 1)
                    elif t == "s1":
                        dve.wait_ge(y_mm, nth(p, 8, 7))
                        if b is not None:
                            dve.wait_ge(xc_done, nth(b, 3, 0))
                        nc.vector.scalar_tensor_tensor(out=s1[:, :], in0=xcur[:, :], scalar=onepD[:, :], in1=psY[:, :],
                                                       op0=ALU.mult, op1=ALU.add).then_inc(s1_done, 1)
                    elif t == "ln":
                        dve.wait_ge(mean_mm, nth(b, 3, i))
                        nc.vector.tensor_tensor(xc[:, :], lnin[i][:, :], psM[:, :], ALU.subtract).then_inc(xc_done, 1)
                        dve.wait_ge(rstd_done, nth(b, 3, i))
                        if i == 2:
                            dve.wait_ge(stored, 16 * b)
                        nc.vector.tensor_tensor(lnout[i][:, :], xc[:, :], rstd[:, :], ALU.mult).then_inc(ln_done, 1)
                    elif t == "kv":
                        dve.wait_ge(k_mm, nth(b, 1, 0))
                        nc.vector.tensor_scalar(kf[:, :], psM[:, 0:MC], w("k_b"), None, ALU.add).then_inc(kf_done, 1)
                        dve.wait_ge(v_mm, nth(b, 5, 4))
                        if b is not None:
                            dve.wait_ge(pv_mm, b * 20)
                        dve.wait_ge(ones_set, 21)

                        def put_v(dst, m, bias):
                            return nc.vector.tensor_tensor(dst, m, bias, ALU.add)

                        def heads(ap):
                            return ap.rearrange("p (h c) -> p h c", c=HD)

                        for g in range(2):
                            for n, i0 in ((7, 0), (1, 7)):
                                o = g * 1024 + i0 * 136
                                c = g * 64 + i0 * HD
                                dst = vp[:, o:o + n * 136] if n > 1 else vp[:, o:o + HD]
                                dst = dst.rearrange("p (h c) -> p h c", c=136)[:, :, 0:HD] if n > 1 else heads(dst)
                                put_v(dst, heads(psM[:, 128 + c:128 + c + n * HD]),
                                      heads(w("v_b", at=c, n=n * HD))).then_inc(v_done, 1)
                        for j in range(4):
                            for r in range(4):
                                rows = slice(32 * j, 32 * j + MREM)
                                o, c = r * 128 + (r % 2) * 32 + j * HD, (4 * r + j) * HD
                                v0 = cols["v_b"][0] + c
                                put_v(vr[rows, o:o + HD], psM[rows, 256 + c:256 + c + HD],
                                      W[rows, v0:v0 + HD]).then_inc(v_done, 1)
                    elif t == "q":
                        dve.wait_ge(q_mm, nth(b, 1, 0))
                        nc.vector.tensor_scalar(qf[:, :], psM[:, :], w("q_b"), SCALE, ALU.add, ALU.mult).then_inc(qf_done, 1)
                    elif t == "mx":
                        c, g = divmod(i, 6)
                        n = min(3, HEADS - 3 * g)
                        dve.wait_ge(sc_mm, nth(b, 24, i))
                        nc.vector.tensor_reduce(mx[:, c, 3 * g:3 * g + n],
                                                psS[i % 2][:, 0:n * MC].rearrange("p (h m) -> p h m", m=MC),
                                                AX.X, ALU.max).then_inc(mx_done, 1)
                    elif t == "mt":
                        dve.wait_ge(mt_mm, nth(b, NT, NT - 1))
                        nc.vector.tensor_scalar(nmf[:, :], psM[0:HEADS, :], -1.0, None, ALU.mult).then_inc(nmf_done, 1)
                    elif t == "on":
                        dve.wait_ge(pv_mm, nth(b, 20, 10 * i + 9))
                        nc.vector.reciprocal(rden[:, i, :], psO[i][64:128, :]).then_inc(rden_done, 1)
                        dve.wait_ge(rden_done, nth(b, 2, i))
                        nc.vector.tensor_tensor(oT[64 * i:64 * i + 64, :], psO[i][0:64, :], rden[:, i, :],
                                                ALU.mult).then_inc(o_done, 1)
                    elif t == "pj":
                        dve.wait_ge(pj_mm, nth(b, 1, 0))
                        nc.vector.scalar_tensor_tensor(out=lnin[1][:, :], in0=psM[:, :], scalar=w("p_b"), in1=lnout[0][:, :],
                                                       op0=ALU.add, op1=ALU.add).then_inc(s2_done, 1)
                    elif t == "ro":
                        done = [0]

                        def link(ins):
                            ins.then_inc(r_step, 1)
                            dve.wait_ge(r_step, nth(b, 13, done[0]))
                            done[0] += 1

                        dve.wait_ge(r_mm, nth(b, NT, NT - 1))
                        logits = psM[:, 0:NT * E].rearrange("p (c e) -> p c e", e=E)
                        link(nc.vector.tensor_reduce(lmx[:, :], logits, AX.X, ALU.max))
                        link(nc.vector.tensor_tensor(lg[:, :, :], logits, per_tile(lmx[:, :]), ALU.subtract))
                        dve.wait_ge(re_done, nth(b, 1, 0))
                        nc.vector.tensor_reduce(psm[:, :], pe_[:, :, :], AX.X, ALU.add)
                        for c in range(NT):
                            last = nc.vector.max(m8[:, c, :], pe_[:, c, :])
                        link(last)
                        nc.vector.reciprocal(prs[:, :], psm[:, :])
                        for c in range(NT):
                            last = nc.vector.max_index(ix[:, c, :], m8[:, c, :], pe_[:, c, :])
                        link(last)
                        link(nc.vector.tensor_copy(ixf[:, :, :], ix[:, :, :]))
                        iota = w("iota").rearrange("p (c e) -> p c e", e=E)
                        for k in range(2):
                            last = nc.vector.tensor_tensor(mk[:, k, :, :], iota, ixf[:, :, k:k + 1].to_broadcast([128, NT, E]),
                                                           ALU.is_equal)
                        link(last)
                        link(nc.vector.tensor_tensor(mks[:, :, :], mk[:, 0, :, :], mk[:, 1, :, :], ALU.add))
                        link(nc.vector.tensor_tensor(wgt[:, :, :], mks[:, :, :], pe_[:, :, :], ALU.mult))
                        link(nc.vector.tensor_tensor(wgn[:, :, :], wgt[:, :, :], per_tile(prs[:, :]), ALU.mult))
                        dve.wait_ge(wt_mm, nth(b, NT, NT - 1))
                        link(nc.vector.tensor_copy(wT[:, :], psM[0:E, :]))
                        link(nc.vector.tensor_copy(ws[0:E, :], wT[:, :]))
                        link(nc.vector.tensor_tensor(wr[:, :], wT[:, :], ws[0:E, :], ALU.subtract))
                        nc.vector.tensor_copy(ws[32:32 + E, :], wr[:, :])
                        link(nc.vector.tensor_copy(wr2[:, :], wr[:, :]))
                        nc.vector.tensor_tensor(ws[64:64 + E, :], wr[:, :], wr2[:, :], ALU.subtract).then_inc(ws_done, 1)
                        assert done[0] == 13
                    elif t == "ex":
                        dve.wait_ge(g_done, nth(b, E, i))
                        dve.wait_ge(wb_mm, nth(b, E, i))
                        if i >= 2:
                            dve.wait_ge(dn_mm, nth(b, E, i - 2))
                        nc.vector.tensor_tensor(gw[:, i % 2, :], gl[:, i % 2, :], psO[i % 2][:, :], ALU.mult).then_inc(gw_done, 1)
                        if i == E - 1:
                            dve.wait_ge(dn_mm, nth(b, E, i))
                            nc.vector.tensor_tensor(lnin[2][:, :], psM[:, :], lnout[1][:, :], ALU.add).then_inc(s3_done, 1)

            run_steps(step, dve.Fori)

        @block.tensor
        def _(pe):
            mm = nc.tensor.matmul
            pe.wait_ge(loaded, 16 * 5)
            pe.wait_ge(consts_set, 4)
            pe.wait_ge(zeroed, 8)
            pe.wait_ge(ones_set, 21)

            def step(p, b):
                def add_pair(k):
                    pe.wait_ge(pair_done, nth(p, 8, k))
                    if k == 0 and b is not None:
                        pe.wait_ge(s1_done, p)
                    mm(psY[:, :], ident, hpair[:, k % 2, :], start=(k == 0), stop=(k == 7)).then_inc(y_mm, 1)

                for t, i in tasks(p, b):
                    if t == "dt1":
                        pe.wait_ge(x_copied, nth(p, 1, 0))
                        if b is not None:
                            pe.wait_ge(s3_done, b)
                        mm(psM[0:R, :], w("w_dt1"), xcur[:, :], start=True, stop=True).then_inc(z1_mm, 1)
                    elif t == "dt2":
                        pe.wait_ge(z1_done, nth(p, 1, 0))
                        mm(psM[:, :], w("w_dt2", R), z1[:, :], start=True, stop=True).then_inc(z2_mm, 1)
                    elif t == "bc":
                        pe.wait_ge(z_done, nth(p, 1, 0))
                        mm(psM[0:96, :], w("w_in3"), xcur[:, :], start=True, stop=True).then_inc(bc_mm, 1)
                        pe.wait_ge(bcs_done, nth(p, 1, 0))
                    elif t == "sc":
                        if i:
                            pe.wait_ge(u_done, nth(p, N, i - 1))
                        mm(psB[:, :], sel[:, i, :], bcs[:, :], start=True, stop=True).then_inc(b_bcast, 1)
                        if i:
                            pe.wait_ge(hc_done, nth(p, N, i - 1))
                        mm(psC[:, :], sel[:, N + i, :], bcs[:, :], start=True, stop=True).then_inc(c_bcast, 1)
                        if i % 2 and i >= 3:
                            add_pair(i // 2 - 1)
                    elif t == "s1":
                        add_pair(7)
                    elif t == "ln":
                        if i == 0:
                            pe.wait_ge(s1_done, nth(b, 1, 0))
                            pe.wait_ge(s3_done, b)
                            if p is not None:
                                pe.wait_ge(bcf_done, nth(p, 1, 0))
                        else:
                            pe.wait_ge((s2_done, s3_done)[i - 1], nth(b, 1, 0))
                        mm(psM[:, :], mean_w[:, :], lnin[i][:, :], start=True, stop=True).then_inc(mean_mm, 1)
                        pe.wait_ge(sq_done, nth(b, 3, i))
                        mm(psM[:, :], mean_w[:, :], sq[:, :], start=True, stop=True).then_inc(var_mm, 1)
                        pe.wait_ge(lnv_done, nth(b, 3, i))
                    elif t == "kv":
                        pe.wait_ge(c_copied, nth(b, 1, 0))
                        mm(psM[:, 0:MC], w("k_w", DC), ccur[:, :], start=True, stop=True).then_inc(k_mm, 1)
                        pe.wait_ge(kf_done, nth(b, 1, 0))
                        mm(psM[:, 128:256], ccur[:, 0:128], w("v_w", DC), start=True, stop=True).then_inc(v_mm, 1)
                        for j in range(4):
                            mm(psM[32 * j:32 * j + MREM, 256:384], ccur[:, 128:MC], w("v_w", DC),
                               start=True, stop=True).then_inc(v_mm, 1)
                    elif t == "q":
                        pe.wait_ge(ln_done, nth(b, 3, 0))
                        pe.wait_ge(v_done, nth(b, 20, 19))
                        mm(psM[:, :], w("q_w"), lnout[0][:, :], start=True, stop=True).then_inc(q_mm, 1)
                    elif t == "mx":
                        c, g = divmod(i, 6)
                        n = min(3, HEADS - 3 * g)
                        if i == 0:
                            pe.wait_ge(q_stacked, nth(b, K_DMAS, K_DMAS - 1))
                            pe.wait_ge(k_stacked, nth(b, K_DMAS, K_DMAS - 1))
                            pe.wait_ge(g_done, b * E)
                        if i >= 2:
                            pe.wait_ge(mx_done, nth(b, 24, i - 2))
                        for h in range(n):
                            last = mm(psS[i % 2][:, h * MC:(h + 1) * MC], qs[0:9 * HD, 3 * g + h, c * 128:(c + 1) * 128],
                                      ks[0:9 * HD, 3 * g + h, 0:MC], start=True, stop=True)
                        last.then_inc(sc_mm, 1)
                    elif t == "mt":
                        pe.wait_ge(mx_done, nth(b, 24, 23))
                        pe.wait_ge(qf_done, nth(b, 1, 0))
                        for c in range(NT):
                            nc.tensor.transpose(psM[0:HEADS, c * 128:(c + 1) * 128], mx[:, c, :], ident).then_inc(mt_mm, 1)
                    elif t == "hd":
                        r, s = ST_ITEMS[i]
                        if i == 0:
                            pe.wait_ge(nm_stacked, nth(b, NM_DMAS, NM_DMAS - 1))
                        if i >= 2:
                            pe.wait_ge(p_done, nth(b, 20, i - 2))
                        if s == 0:
                            for j in range(4):
                                last = mm(psS[i % 2][32 * j:32 * j + MPAD, :], ks[:, 4 * r + j, 128:128 + MPAD],
                                          qs[:, 4 * r + j, :], start=True, stop=True)
                        else:
                            h = 4 * r + s - 1
                            last = mm(psS[i % 2][:, :], ks[:, h, 0:128], qs[:, h, :], start=True, stop=True)
                        last.then_inc(st_mm, 1)
                    elif t == "pv":
                        r, s = ST_ITEMS[i]
                        g = i // 10
                        if i == 0:
                            pe.wait_ge(v_done, nth(b, 20, 19))
                            pe.wait_ge(gw_done, b * E)
                        pe.wait_ge(p_done, nth(b, 20, i))
                        vals = vr[:, r * 128:(r + 1) * 128] if s == 0 else vp[:, (4 * r + s - 1) * 128:(4 * r + s) * 128]
                        mm(psO[g][:, :], vals, pt[:, i % 3, :], start=(i % 10 == 0), stop=(i % 10 == 9)).then_inc(pv_mm, 1)
                    elif t == "pj":
                        pe.wait_ge(o_done, nth(b, 2, 1))
                        pe.wait_ge(nmf_done, nth(b, 1, 0))
                        mm(psM[:, :], w("p_w"), oT[:, :], start=True, stop=True).then_inc(pj_mm, 1)
                    elif t == "ro":
                        pe.wait_ge(ln_done, nth(b, 3, 1))
                        for c in range(NT):
                            mm(psM[:, c * E:(c + 1) * E], lnout[1][:, c * 128:(c + 1) * 128], w("r_w"),
                               start=True, stop=True).then_inc(r_mm, 1)
                        pe.wait_ge(r_step, nth(b, 13, 8))
                        for c in range(NT):
                            nc.tensor.transpose(psM[0:E, c * 128:(c + 1) * 128], wgn[:, c, :], ident).then_inc(wt_mm, 1)
                    elif t == "ex":
                        if i == 0:
                            pe.wait_ge(r_step, nth(b, 13, 9))
                            mm(psM[:, :], w("e_bout", E), wT[:, :], start=True, stop=False)

                        def up(e):
                            if e >= 2:
                                pe.wait_ge(g_done, nth(b, E, e - 2))
                            else:
                                pe.wait_ge(p_done, nth(b, 20, 18 + e))
                            mm(psS[e % 2][:, :], w("e_win", at=e * D, n=D), lnout[1][:, :], start=True, stop=True).then_inc(up_mm, 1)
                            if e >= 2:
                                pe.wait_ge(gw_done, nth(b, E, e - 2))
                            else:
                                pe.wait_ge(ws_done, nth(b, 1, 0))
                            mm(psO[e % 2][:, :], sel[:, e, :], ws[:, :], start=True, stop=True).then_inc(wb_mm, 1)

                        def down(e):
                            pe.wait_ge(gw_done, nth(b, E, e))
                            mm(psM[:, :], w("e_wout", at=e * D, n=D), gw[:, e % 2, :], start=False,
                               stop=(e == E - 1)).then_inc(dn_mm, 1)

                        up(i)
                        if i:
                            down(i - 1)
                        if i == E - 1:
                            down(i)

            run_steps(step, pe.Fori)


def kernel(**inputs):
    import numpy as _np
    import concourse.bacc as _bacc
    from concourse import mybir as _mybir
    from concourse.bass_utils import run_bass_kernel_spmd as _run

    x = {k: _np.asarray(v) for k, v in inputs.items()}
    cols, width = pack_layout()
    pack = _np.zeros((128, width), _np.float32)

    def put(name, a):
        first, n = cols[name]
        pack[0:a.shape[0], first:first + n] = a

    dh = _np.arange(D).reshape(HEADS, HD).T.reshape(-1)
    kv_w, kv_b = x["L0_xattn_kv_w"], x["L0_xattn_kv_b"]
    put("w_in3", _np.tile(x["L0_attn_W_in"], (1, 3)))
    put("w_dt1", x["L0_attn_W_dt1"])
    put("w_dt2", x["L0_attn_W_dt2"])
    put("A", x["L0_attn_A"].reshape(D, N))
    put("D", x["L0_attn_D"].reshape(D, 1))
    put("b_dt2", x["L0_attn_b_dt2"].reshape(D, 1))
    put("b_dt1", x["L0_attn_b_dt1"].reshape(R, 1))
    put("b_in3", _np.tile(x["L0_attn_b_in"], 3).reshape(96, 1))
    put("eye3", _np.tile(_np.eye(32, dtype=_np.float32), (3, 1)))
    put("ident", _np.eye(128, dtype=_np.float32))
    put("iota", _np.tile(_np.arange(E, dtype=_np.float32), (128, NT)))
    put("q_w", x["L0_xattn_q_w"][:, dh])
    put("q_b", x["L0_xattn_q_b"][dh].reshape(D, 1))
    put("k_w", kv_w[:, 0:D][:, dh])
    put("k_b", kv_b[0:D][dh].reshape(D, 1))
    put("v_w", kv_w[:, D:2 * D])
    put("v_b", _np.tile(kv_b[D:2 * D].reshape(1, D), (128, 1)))
    put("p_w", x["L0_xattn_proj_w"])
    put("p_b", x["L0_xattn_proj_b"].reshape(D, 1))
    put("r_w", x["L0_ffn_router_w"])
    put("e_bin", x["L0_ffn_b_in"].T)
    put("e_bout", x["L0_ffn_b_out"])
    put("e_win", x["L0_ffn_w_in"].transpose(1, 0, 2).reshape(D, E * D))
    put("e_wout", x["L0_ffn_w_out"].transpose(1, 0, 2).reshape(D, E * D))
    arrays = {
        "in_xT": _np.ascontiguousarray(x["x"].transpose(2, 0, 1)),
        "in_ctxT": _np.ascontiguousarray(x["ctx_768"].transpose(2, 0, 1)),
        "in_pack": pack,
    }
    nc = _bacc.Bacc("TRN2", target_bir_lowering=False, num_devices=1)
    args = [nc.dram_tensor(n, a.shape, _mybir.dt.from_np(a.dtype), kind="ExternalInput").ap() for n, a in arrays.items()]
    args.append(nc.dram_tensor("out_T", (B, D, L), _mybir.dt.float32, kind="ExternalOutput").ap())
    decoder_block(nc, *args)
    r = _run(nc, [arrays], core_ids=[0])
    return _np.ascontiguousarray(r.results[0]["out_T"].transpose(0, 2, 1))
```

```python
import concourse.bass as bass
from concourse import mybir
from contextlib import ExitStack

B, L, D, N, R = 4, 512, 128, 16, 64
HEADS, HD = 16, 8
MC, DC = 154, 96
MREM = MC - 128
MPAD = 32
E, NT = 8, L // 128
DT_MIN, DT_MAX, EPS = 1e-7, 1e6, 1e-5
SCALE = float(HD) ** -0.5
MAXROW = 96
KS = MAXROW + 3


def pack_layout():
    widths = [("w_in3", 96), ("w_dt1", R), ("w_dt2", D), ("A", N), ("D", 1), ("b_dt2", 1), ("b_dt1", 1),
              ("b_in3", 1), ("eye3", 32), ("ident", 128), ("iota", NT * E),
              ("q_w", D), ("q_b", 1), ("k_w", D), ("k_b", 1), ("v_w", D), ("v_b", D), ("p_w", D), ("p_b", 1),
              ("r_w", E), ("e_bin", E), ("e_bout", D), ("e_win", E * D), ("e_wout", E * D)]
    at, out = 0, {}
    for name, w in widths:
        out[name] = (at, w)
        at += w
    return out, at


ST_ITEMS = [(r, s) for r in range(4) for s in range(5)]
N_ST = len(ST_ITEMS)
N_ABAR = 8
MX_GROUPS = -(-HEADS // 3)


def plan():
    tasks = []

    def add(stage, at, engine, name, i=0):
        tasks.append((at, len(tasks), engine, stage, name, i))

    for q, at in enumerate((-30, 10, 24, 40)):
        for d, engine, name in (
                (0, "pe", "z1"), (1, "act", "z1"), (2, "pe", "z2"), (2.2, "pe", "bc"), (3, "act", "z"), (2.6, "act", "bc"),
                (4, "act", "softplus"), (5, "pool", "bc_rest"), (6, "dve", "dt"), (6, "act", "bc_second"),
                (7, "dve", "bc_third")):
            add(0, at + d, engine, name, q)

    scan_at = [3, 6.5, 10, 13, 20, 28] + [38 + 2.9 * k for k in range(10)]
    add(1, -3, "dve", "cur")
    for n, t in enumerate(scan_at):
        ahead = scan_at[n - 2] if n >= 2 else -2 + 2 * n
        add(1, ahead - 0.8, "pe", "b_bcast", n)
        add(1, ahead - 0.4, "act", "b_copy", n)
        add(1, ahead, "pool", "u", n)
        add(1, min(ahead, 1.9 * n - 1) if n < 8 else ahead, "act", "a_bar", n)
        add(1, t - 1, "pe", "c_bcast", n)
        add(1, t - 0.1 if n == 0 else scan_at[n - 1] + 0.1, "dve", "bbar", n)
        add(1, t, "dve", "scan", n)
        add(1, t + 0.2, "dve", "hc", n)
        if n % 2:
            add(1, t + 1.5, "pool", "pair", n // 2)
            add(1, t + 4, "pe", "y", n // 2)
    add(1, 69, "dve", "s1")

    def norm(stage, k, at):
        for d, engine, name in ((0, "pe", "mean"), (1, "dve", "centre"), (1.7, "act", "square"), (2.4, "pe", "var"),
                                (3.4, "act", "rstd"), (5, "dve", "norm")):
            add(stage, at + d, engine, name, k)

    def parts(at, what):
        for d, engine, name in ((0, "act", "first"), (0.7, "pool", "rest"), (2, "act", "second"), (2.7, "pool", "third")):
            add(2, at + d, engine, name, what)

    norm(2, 0, 0)
    add(2, -1, "pool", "ctx")
    add(2, 1, "pe", "kv")
    add(2, 2, "dve", "k")
    add(2, 2.3, "dve", "v")
    parts(3, "k")
    add(2, 6, "pe", "q")
    add(2, 7, "dve", "q")
    parts(7.7, "q")
    for g in range(NT * MX_GROUPS):
        add(2, 15.5 + 0.87 * g, "pe", "mx", g)
        add(2, 16 + 0.87 * g, "dve", "mx", g)
    add(2, 37, "pe", "mt")
    add(2, 37.5, "dve", "mt")
    parts(38.3, "m")
    for j in range(N_ST):
        add(2, 43 + 1.15 * j, "pe", "st", j)
        add(2, 43.5 + 1.15 * j, "act", "p", j)
        add(2, 44.8 + 1.15 * j, "pe", "pv", j)
    for g, at in ((0, 56.5), (1, 68)):
        add(2, at, "act", "rden", g)
        add(2, at + 1, "dve", "o", g)
    add(2, 69.5, "pe", "proj")
    add(2, 70.5, "dve", "s2")

    norm(3, 1, 0.6)
    add(3, 6.8, "pe", "logits")
    add(3, 7.3, "dve", "logits")
    add(3, 7.6, "act", "router_exp")
    add(3, 8.2, "dve", "router")
    add(3, 11.3, "pe", "wt")
    add(3, 11.8, "act", "w_first")
    add(3, 13, "pool", "w_rest")
    add(3, 14.3, "act", "w_second")
    add(3, 15.4, "dve", "w_third")
    add(3, 16.3, "act", "gelu_table")
    for e in range(E):
        at = 17 + 2.4 * e
        add(3, at, "pe", "up", e)
        add(3, at + 0.8, "act", "gelu", e)
        add(3, at + 1.5, "dve", "gate", e)
        add(3, at + 2.6, "pe", "down", e)
    add(3, 36.8, "dve", "s3")
    add(3, 36.5, "act", "exp_table")
    norm(3, 2, 39.5)
    tasks.sort()
    return {e: [(stage, name, i) for _, _, f, stage, name, i in tasks if f == e] for e in ("pe", "act", "dve", "pool")}


PLAN = plan()


def decoder_block(nc, xT, ctxT, wpack, out):
    F32, BF16, U32 = mybir.dt.float32, mybir.dt.bfloat16, mybir.dt.uint32
    ALU, ACT, AX = mybir.AluOpType, mybir.ActivationFunctionType, mybir.AxisListType
    cols, WC = pack_layout()
    ctx = ExitStack()
    with ctx:
        def sb(name, shape, dt=F32):
            return ctx.enter_context(nc.sbuf_tensor(name, shape, dt))

        def sem(name):
            return ctx.enter_context(nc.semaphore(name))

        W = sb("W", [128, WC])
        xall = sb("xall", [128, B, L])
        call = sb("call", [DC, B, MC])
        consts = sb("consts", [128, 2])
        sel = sb("sel", [96, 32, 128], BF16)
        mean_w = sb("mean_w", [128, 128])
        onepD = sb("onepD", [128, 1])
        rA = sb("rA", [128, N])
        dtall = sb("dtall", [128, B, L])
        bcsall = sb("bcsall", [96, B, L], BF16)
        xcur = sb("xcur", [128, L])
        z1 = sb("z1", [R, L])
        z = sb("z", [128, L])
        zlog = sb("zlog", [128, L])
        dt = sb("dt", [128, L])
        bcf = sb("bcf", [96, L])
        bcr = sb("bcr", [96, L])
        bct = sb("bct", [96, L], BF16)
        bcs = sb("bcs", [96, L], BF16)
        bsb = sb("bsb", [128, 2, L])
        abar = sb("abar", [128, N_ABAR, L])
        ub = sb("ub", [128, 4, L])
        bbar = sb("bbar", [128, 2, L])
        hst = sb("hst", [128, 2, L])
        hc = sb("hc", [128, 4, L])
        hpair = sb("hpair", [128, 2, L])
        lnin = [sb(f"s{k + 1}", [128, L]) for k in range(3)]
        x1, x2, x3 = sb("x1", [128, L]), sb("x2", [128, L]), sb("x3", [128, B, L])
        xc = [sb(f"xc{k + 1}", [128, L]) for k in range(3)]
        rstd = [sb(f"rstd{k + 1}", [128, L]) for k in range(3)]
        ccur = sb("ccur", [DC, MC])
        kf = sb("kf", [128, MC])
        kr = sb("kr", [128, MC])
        kp = [sb(f"kp{j}", [128, 128 + MPAD], BF16) for j in range(3)]
        qf = sb("qf", [128, L])
        qr = sb("qr", [128, L])
        qp = [sb(f"qp{j}", [128, L], BF16) for j in range(3)]
        ks = sb("ks", [KS, HEADS, 128 + MPAD], BF16)
        qs = sb("qs", [KS, HEADS, L], BF16)
        vp = sb("vp", [128, HEADS * 128 + 64])
        vr = sb("vr", [128, 4 * 128 + 64])
        mx = sb("mx", [128, NT, HEADS])
        nmf = z[0:HEADS, :]
        nmr = bcf[0:HEADS, :]
        nmp = [sb(f"nmp{j}", [HEADS, L], BF16) for j in range(3)]
        pt = sb("pt", [128, 3, L])
        rden = sb("rden", [64, 2, L])
        oT = sb("oT", [128, L])
        lmx = sb("lmx", [128, NT])
        lg = sb("lg", [128, NT, E])
        pe_ = sb("pe_", [128, NT, E])
        psm = sb("psm", [128, NT])
        prs = sb("prs", [128, NT])
        m8 = sb("m8", [128, NT, 8])
        ix = sb("ix", [128, NT, 8], U32)
        ixf = sb("ixf", [128, NT, 8])
        mk = sb("mk", [128, 2, NT, E])
        mks = sb("mks", [128, NT, E])
        wgt = sb("wgt", [128, NT, E])
        wgn = sb("wgn", [128, NT, E])
        wT = z1[0:E, :]
        wr = zlog[0:E, :]
        wr2 = sb("wr2", [E, L], BF16)
        ws = sb("ws", [96, L], BF16)
        gl = sb("gl", [128, 2, L])

        def ps(name):
            return ctx.enter_context(nc.psum_tensor(name, [128, 512], F32))

        psB, psC, psY, psS0, psS1, psO, psX, psM = [ps(n) for n in ("psB", "psC", "psY", "psS0", "psS1", "psO", "psX", "psM")]
        psS, psH = [psS0, psS1], [psO, psX]

        def w(name, rows=128, at=0, n=None):
            first, width = cols[name]
            return W[0:rows, first + at:first + at + (width if n is None else n)]

        ident = w("ident")

        def sems(names):
            return [sem(n) for n in names.split()]

        w1_loaded, w2_loaded, x0_loaded, xr_loaded, c_loaded, consts_set, sel_set, inv_done, zeroed, ones_set, stored = sems(
            "w1_loaded w2_loaded x0_loaded xr_loaded c_loaded consts_set sel_set inv_done zeroed ones_set stored")
        z1_mm, z1_done, z2_mm, z_done, zabs_done, zexp_done, zlog_done, dtr_done, dt_done = sems(
            "z1_mm z1_done z2_mm z_done zabs_done zexp_done zlog_done dtr_done dt_done")
        bc_mm, bcf_done, bc_first, bcr_done, bc_second, bcs_done = sems(
            "bc_mm bcf_done bc_first bcr_done bc_second bcs_done")
        cur_done, s1_done, pair_done, y_mm = sems("cur_done s1_done pair_done y_mm")
        b_mm, b_done, c_mm, a_done, u_done, bb_done, h_done, hc_done = sems(
            "b_mm b_done c_mm a_done u_done bb_done h_done hc_done")
        mean_mm, xc_done, sq_done, var_mm, lnv_done, rstd_done, ln_done = [
            [sem(f"{n}{k}") for k in range(3)] for n in "mean_mm xc_done sq_done var_mm lnv_done rstd_done ln_done".split()]
        c_copied, v_mm, kf_done, v_done, q_mm, qf_done = sems("c_copied v_mm kf_done v_done q_mm qf_done")
        first, rest, second, third = [{w_: sem(f"{n}_{w_}") for w_ in "kqm"} for n in ("first", "rest", "second", "third")]
        k_stacked, q_stacked, m_stacked = sems("k_stacked q_stacked m_stacked")
        sc_mm, mx_done, mt_mm, nmf_done = sems("sc_mm mx_done mt_mm nmf_done")
        st_mm, p_done, pv_mm, lden_done, rden_done, o_done, pj_mm, s2_done = sems(
            "st_mm p_done pv_mm lden_done rden_done o_done pj_mm s2_done")
        r_mm, lmx_done, lg_done, re_done, max_done, ix_done, ixf_done, mk_done, mks_done, wgt_done, wgn_done = sems(
            "r_mm lmx_done lg_done re_done max_done ix_done ixf_done mk_done mks_done wgt_done wgn_done")
        wt_mm, w_first, w_rest, w_second, ws_done = sems("wt_mm w_first w_rest w_second ws_done")
        up_mm, wb_mm, g_done, gw_done, dn_mm, s3_done = sems("up_mm wb_mm g_done gw_done dn_mm s3_done")

        N_MX = NT * MX_GROUPS

        def nth(batch, i=0, per_batch=1):
            return batch * per_batch + i + 1

        def wait_earlier(eng, what, batch, i, per_batch, lag):
            value = batch * per_batch + i + 1 - lag
            if not isinstance(batch, int) or value > 0:
                eng.wait_ge(what, value)

        def run_steps(walk, fori):
            walk(0, None, None)
            walk(1, 0, None)
            with fori(0, B - 2) as c:
                walk(c + 2, c + 1, c)
            walk(None, B - 1, B - 2)
            walk(None, None, B - 1)

        def step_tasks(engine, p, b, c):
            batch = {0: p if isinstance(p, int) and p == 0 else None, 1: p, 2: b, 3: c}
            return [(name, i, batch[stage]) for stage, name, i in PLAN[engine] if batch[stage] is not None]

        block = ctx.enter_context(nc.Block())

        @block.sync
        def _(sp):
            split = cols["q_w"][0]
            sp.dma_start(W[:, 0:split], wpack[:, 0:split]).then_inc(w1_loaded, 16)
            sp.dma_start(xall[:, 0, :], xT[:, 0, :]).then_inc(x0_loaded, 16)
            sp.dma_start(xall[:, 1:B, :], xT[:, 1:B, :]).then_inc(xr_loaded, 16)
            sp.dma_start(call[:, :, :], ctxT).then_inc(c_loaded, 16)
            sp.dma_start(W[:, split:WC], wpack[:, split:WC]).then_inc(w2_loaded, 16)
            sp.wait_ge(ones_set, 17)

            def walk(p, b, c):
                if b is not None:
                    for j, part in enumerate((first, second, third)):
                        sp.wait_ge(part["k"], nth(b))
                        for i in range(3):
                            row = (i * 3 + j) * HD
                            sp.dma_start(ks[row:row + HD, :, :], kp[j][:, :]).then_inc(k_stacked, 16)
                    for i, part in enumerate((first, second, third)):
                        sp.wait_ge(part["q"], nth(b))
                        for j in range(3):
                            row = (i * 3 + j) * HD
                            sp.dma_start(qs[row:row + HD, :, :], qp[i][:, :]).then_inc(q_stacked, 16)
                    for j, part in enumerate((first, second, third)):
                        sp.wait_ge(part["m"], nth(b))
                        sp.dma_start(qs[MAXROW + j:MAXROW + j + 1, :, :], nmp[j][:, :]).then_inc(m_stacked, 16)
                if c is not None:
                    sp.wait_ge(ln_done[2], nth(c))
                    sp.dma_start(out[bass.ds(c, 1), :, :], x3[:, bass.ds(c, 1), :]).then_inc(stored, 16)

            run_steps(walk, sp.Fori)
            sp.wait_ge(stored, 16 * B)

        @block.gpsimd
        def _(pool):
            pool.memset(consts[:, 0:1], EPS).then_inc(consts_set, 1)
            pool.memset(consts[:, 1:2], 1.0).then_inc(consts_set, 1)
            pool.memset(mean_w[:, :], 1.0 / D).then_inc(consts_set, 1)
            pool.wait_ge(w1_loaded, 16)
            pool.tensor_copy(sel[:, :, :], w("eye3", 96).unsqueeze(2).to_broadcast([96, 32, 128])).then_inc(sel_set, 1)

            whole_of = {"k": (kf[:, :], kr[:, :], [t[:, 0:MC] for t in kp], kf_done),
                        "q": (qf[:, :], qr[:, :], [t[:, :] for t in qp], qf_done),
                        "m": (nmf, nmr, [t[:, :] for t in nmp], nmf_done)}

            def walk(p, b, c):
                for t, i, batch in step_tasks("pool", p, b, c):
                    if t == "bc_rest":
                        pool.wait_ge(bc_first, nth(i))
                        pool.wait_ge(bcf_done, nth(i))
                        pool.tensor_tensor(bcr[:, :], bcf[:, :], bcsall[:, i, :], ALU.subtract).then_inc(bcr_done, 1)
                    elif t == "u":
                        if i == 0:
                            pool.wait_ge(cur_done, nth(p))
                        wait_earlier(pool, bb_done, p, i, N, 4)
                        pool.wait_ge(b_done, nth(p, i, N))
                        pool.tensor_tensor(ub[:, i % 4, :], bsb[:, i % 2, :], xcur[:, :], ALU.mult).then_inc(u_done, 1)
                    elif t == "pair":
                        pool.wait_ge(hc_done, nth(p, 2 * i + 1, N))
                        wait_earlier(pool, y_mm, p, i, N // 2, 2)
                        pool.tensor_tensor(hpair[:, i % 2, :], hc[:, 2 * i % 4, :], hc[:, (2 * i + 1) % 4, :],
                                           ALU.add).then_inc(pair_done, 1)
                    elif t == "ctx":
                        pool.wait_ge(c_loaded, 16)
                        pool.tensor_copy(ccur[:, :], call[:, bass.ds(b, 1), :]).then_inc(c_copied, 1)
                    elif t == "rest":
                        whole, left, parts, whole_done = whole_of[i]
                        pool.wait_ge(first[i], nth(b))
                        pool.tensor_tensor(left, whole, parts[0], ALU.subtract).then_inc(rest[i], 1)
                    elif t == "third":
                        whole, left, parts, whole_done = whole_of[i]
                        pool.wait_ge(second[i], nth(b))
                        pool.tensor_tensor(parts[2], left, parts[1], ALU.subtract).then_inc(third[i], 1)
                    elif t == "w_rest":
                        pool.wait_ge(w_first, nth(c))
                        pool.tensor_tensor(wr, wT, ws[0:E, :], ALU.subtract).then_inc(w_rest, 1)
                    else:
                        assert False, t

            run_steps(walk, pool.Fori)

        @block.scalar
        def _(act):
            eps, one = consts[:, 0:1], consts[:, 1:2]
            whole_of = {"k": (kf[:, :], kr[:, :], [t[:, 0:MC] for t in kp], kf_done),
                        "q": (qf[:, :], qr[:, :], [t[:, :] for t in qp], qf_done),
                        "m": (nmf, nmr, [t[:, :] for t in nmp], nmf_done)}
            nc.scalar.preload_act_table_set("natural_log_exp_and_others")
            act.wait_ge(w1_loaded, 16)
            act.wait_ge(consts_set, 3)

            def walk(p, b, c):
                if p is None or not isinstance(p, int) or p:
                    nc.scalar.preload_act_table_set("natural_log_exp_and_others")
                for t, i, batch in step_tasks("act", p, b, c):
                    if t == "z1":
                        act.wait_ge(z1_mm, nth(i))
                        nc.scalar.activation(z1[:, :], psM[0:R, :], ACT.Identity, bias=w("b_dt1", R)).then_inc(z1_done, 1)
                    elif t == "z":
                        act.wait_ge(z2_mm, nth(i))
                        wait_earlier(act, dtr_done, i, 0, 1, 1)
                        nc.scalar.activation(z[:, :], psM[:, :], ACT.Identity, bias=w("b_dt2")).then_inc(z_done, 1)
                    elif t == "softplus":
                        act.wait_ge(z_done, nth(i))
                        nc.scalar.activation(zlog[:, :], z[:, :], ACT.Abs).then_inc(zabs_done, 1)
                        act.wait_ge(zabs_done, nth(i))
                        nc.scalar.activation(zlog[:, :], zlog[:, :], ACT.Exp, scale=-1.0).then_inc(zexp_done, 1)
                        act.wait_ge(zexp_done, nth(i))
                        nc.scalar.activation(zlog[:, :], zlog[:, :], ACT.Ln, bias=one).then_inc(zlog_done, 1)
                    elif t == "bc":
                        act.wait_ge(bc_mm, nth(i))
                        wait_earlier(act, bcs_done, i, 0, 1, 1)
                        nc.scalar.activation(bcf[:, :], psB[0:96, :], ACT.Identity, bias=w("b_in3", 96)).then_inc(bcf_done, 1)
                        nc.scalar.activation(bcsall[:, i, :], psB[0:96, :], ACT.Identity, bias=w("b_in3", 96)).then_inc(bc_first, 1)
                    elif t == "bc_second":
                        act.wait_ge(bcr_done, nth(i))
                        nc.scalar.copy(bct[64:96, :], bcr[64:96, :])
                        nc.scalar.copy(bcsall[32:64, i, :], bcr[32:64, :]).then_inc(bc_second, 1)
                    elif t == "b_copy":
                        act.wait_ge(b_mm, nth(p, i, N))
                        wait_earlier(act, u_done, p, i, N, 2)
                        nc.scalar.copy(bsb[:, i % 2, :], psB[:, :]).then_inc(b_done, 1)
                    elif t == "a_bar":
                        if i == 0:
                            act.wait_ge(cur_done, nth(p))
                        wait_earlier(act, h_done, p, i, N, N_ABAR)
                        nc.scalar.activation(abar[:, i % N_ABAR, :], dt[:, :], ACT.Exp, scale=w("A", at=i, n=1)).then_inc(a_done, 1)
                    elif t == "square":
                        act.wait_ge(xc_done[i], nth(batch))
                        nc.scalar.activation(rstd[i][:, :], xc[i][:, :], ACT.Square).then_inc(sq_done[i], 1)
                    elif t == "rstd":
                        act.wait_ge(var_mm[i], nth(batch))
                        bank = psX if i == 1 else psM
                        nc.scalar.activation(rstd[i][:, :], bank[:, :], ACT.Ln, bias=eps).then_inc(lnv_done[i], 1)
                        act.wait_ge(lnv_done[i], nth(batch))
                        nc.scalar.activation(rstd[i][:, :], rstd[i][:, :], ACT.Exp, scale=-0.5).then_inc(rstd_done[i], 1)
                    elif t == "first":
                        whole, left, parts, whole_done = whole_of[i]
                        if i == "k":
                            act.wait_ge(zeroed, 6)
                        act.wait_ge(whole_done, nth(b))
                        nc.scalar.copy(parts[0], whole).then_inc(first[i], 1)
                    elif t == "second":
                        whole, left, parts, whole_done = whole_of[i]
                        act.wait_ge(rest[i], nth(b))
                        nc.scalar.copy(parts[1], left).then_inc(second[i], 1)
                    elif t == "p":
                        act.wait_ge(st_mm, nth(b, i, N_ST))
                        if i >= 3:
                            act.wait_ge(pv_mm, nth(b, i - 3, N_ST))
                        nc.scalar.activation(pt[:, i % 3, :], psS[i % 2][:, :], ACT.Exp).then_inc(p_done, 1)
                    elif t == "rden":
                        act.wait_ge(pv_mm, nth(b, (i + 1) * N_ST // 2 - 1, N_ST))
                        nc.scalar.activation(rden[:, i, :], psH[i][64:128, :], ACT.Ln).then_inc(lden_done, 1)
                        act.wait_ge(lden_done, nth(b, i, 2))
                        nc.scalar.activation(rden[:, i, :], rden[:, i, :], ACT.Exp, scale=-1.0).then_inc(rden_done, 1)
                    elif t == "router_exp":
                        act.wait_ge(lg_done, nth(c))
                        nc.scalar.activation(pe_[:, :, :], lg[:, :, :], ACT.Exp).then_inc(re_done, 1)
                    elif t == "w_first":
                        act.wait_ge(wt_mm, nth(c, NT - 1, NT))
                        nc.scalar.copy(wT, psX[0:E, :])
                        nc.scalar.copy(ws[0:E, :], psX[0:E, :]).then_inc(w_first, 1)
                    elif t == "w_second":
                        act.wait_ge(w_rest, nth(c))
                        nc.scalar.copy(ws[32:32 + E, :], wr)
                        nc.scalar.copy(wr2[:, :], wr).then_inc(w_second, 1)
                    elif t == "gelu_table":
                        nc.scalar.preload_act_table(ACT.Gelu_apprx_tanh)
                    elif t == "exp_table":
                        nc.scalar.preload_act_table_set("natural_log_exp_and_others")
                    elif t == "gelu":
                        act.wait_ge(up_mm, nth(c, i, E))
                        if i >= 2:
                            act.wait_ge(dn_mm, nth(c, i - 2, E))
                        nc.scalar.activation(gl[:, i % 2, :], psX[:, :], ACT.Gelu_apprx_tanh,
                                             bias=w("e_bin", at=i, n=1)).then_inc(g_done, 1)
                    else:
                        assert False, t

            run_steps(walk, act.Fori)

        @block.vector
        def _(dve):
            nc.vector.memset(ks[:, :, :].rearrange("p h m -> p (h m)").bitcast(U32), 0).then_inc(zeroed, 1)
            nc.vector.memset(vr[:, :], 0.0).then_inc(zeroed, 1)
            nc.vector.memset(ws[:, :].bitcast(U32), 0).then_inc(zeroed, 1)
            for t in kp:
                nc.vector.memset(t[:, :].bitcast(U32), 0).then_inc(zeroed, 1)
            nc.vector.memset(vp[:, :], 0.0).then_inc(zeroed, 1)
            nc.vector.memset(qs[64:96, :, :].rearrange("p h m -> p (h m)").bitcast(U32), 0).then_inc(zeroed, 1)
            dve.wait_ge(zeroed, 8)
            nc.vector.memset(ks[MAXROW:KS, :, 0:MC], 1.0).then_inc(ones_set, 1)

            def every_136(tile, rows, at, n):
                if n == 1:
                    return tile[rows, at:at + HD].rearrange("p (h c) -> p h c", c=HD)
                return tile[rows, at:at + n * 136].rearrange("p (h c) -> p h c", c=136)[:, :, 0:HD]

            everything = slice(0, 128)
            for g in range(2):
                for n, i0 in ((7, 0), (1, 7)):
                    nc.vector.memset(every_136(vp, everything, g * 1024 + i0 * 136 + 64, n), 1.0)
            for j in range(4):
                for r in range(4):
                    o = r * 128 + (r % 2) * 32 + j * HD + 64
                    nc.vector.memset(vr[32 * j:32 * j + MREM, o:o + HD], 1.0).then_inc(ones_set, 1)
            dve.wait_ge(w1_loaded, 16)
            nc.vector.reciprocal(rA[:, :], w("A")).then_inc(inv_done, 1)
            nc.vector.tensor_scalar(onepD[:, :], w("D"), 1.0, None, ALU.add).then_inc(inv_done, 1)
            dve.wait_ge(inv_done, 2)

            def per_tile(ap):
                return ap.unsqueeze(2).to_broadcast([128, NT, E])

            def heads(ap):
                return ap.rearrange("p (h c) -> p h c", c=HD)

            def walk(p, b, c):
                for t, i, batch in step_tasks("dve", p, b, c):
                    if t == "dt":
                        dve.wait_ge(zlog_done, nth(i))
                        nc.vector.scalar_tensor_tensor(out=dtall[:, i, :], in0=z[:, :], scalar=0.0, in1=zlog[:, :],
                                                       op0=ALU.max, op1=ALU.add).then_inc(dtr_done, 1)
                        dve.wait_ge(dtr_done, nth(i))
                        nc.vector.tensor_scalar(dtall[:, i, :], dtall[:, i, :], DT_MIN, DT_MAX, ALU.max, ALU.min).then_inc(dt_done, 1)
                    elif t == "bc_third":
                        dve.wait_ge(bc_second, nth(i))
                        nc.vector.tensor_tensor(bcsall[64:96, i, :], bcr[64:96, :], bct[64:96, :], ALU.subtract).then_inc(bcs_done, 1)
                    elif t == "cur":
                        if isinstance(p, int):
                            dve.wait_ge(xr_loaded if p else x0_loaded, 16)
                            dve.wait_ge(dt_done, nth(p))
                            dve.wait_ge(bcs_done, nth(p))
                        wait_earlier(dve, s1_done, p, 0, 1, 1)
                        nc.vector.tensor_copy(bcs[:, :], bcsall[:, bass.ds(p, 1), :])
                        nc.vector.tensor_copy(dt[:, :], dtall[:, bass.ds(p, 1), :])
                        nc.vector.tensor_copy(xcur[:, :], xall[:, bass.ds(p, 1), :]).then_inc(cur_done, 1)
                    elif t == "bbar":
                        dve.wait_ge(u_done, nth(p, i, N))
                        dve.wait_ge(a_done, nth(p, i, N))
                        nc.vector.scalar_tensor_tensor(out=bbar[:, i % 2, :], in0=abar[:, i % N_ABAR, :], scalar=-1.0, in1=ub[:, i % 4, :],
                                                       op0=ALU.add, op1=ALU.mult).then_inc(bb_done, 1)
                    elif t == "scan":
                        dve.wait_ge(bb_done, nth(p, i, N))
                        nc.vector.tensor_tensor_scan(hst[:, i % 2, :], abar[:, i % N_ABAR, :], bbar[:, i % 2, :], 0.0,
                                                     ALU.mult, ALU.add).then_inc(h_done, 1)
                    elif t == "hc":
                        dve.wait_ge(h_done, nth(p, i, N))
                        dve.wait_ge(c_mm, nth(p, i, N))
                        wait_earlier(dve, pair_done, p, i // 2, N // 2, 2)
                        nc.vector.scalar_tensor_tensor(out=hc[:, i % 4, :], in0=hst[:, i % 2, :], scalar=rA[:, i:i + 1],
                                                       in1=psC[:, :], op0=ALU.mult, op1=ALU.mult).then_inc(hc_done, 1)
                    elif t == "s1":
                        dve.wait_ge(y_mm, nth(p, N // 2 - 1, N // 2))
                        nc.vector.scalar_tensor_tensor(out=lnin[0][:, :], in0=xcur[:, :], scalar=onepD[:, :], in1=psY[:, :],
                                                       op0=ALU.mult, op1=ALU.add).then_inc(s1_done, 1)
                    elif t == "centre":
                        dve.wait_ge(mean_mm[i], nth(batch))
                        bank = psX if i == 1 else psM
                        nc.vector.tensor_tensor(xc[i][:, :], lnin[i][:, :], bank[:, :], ALU.subtract).then_inc(xc_done[i], 1)
                    elif t == "norm":
                        dve.wait_ge(rstd_done[i], nth(batch))
                        dst = (x1[:, :], x2[:, :], x3[:, bass.ds(batch, 1), :])[i]
                        nc.vector.tensor_tensor(dst, xc[i][:, :], rstd[i][:, :], ALU.mult).then_inc(ln_done[i], 1)
                    elif t == "k":
                        dve.wait_ge(v_mm, nth(b))
                        nc.vector.tensor_scalar(kf[:, :], psO[:, 0:MC], w("k_b"), None, ALU.add).then_inc(kf_done, 1)
                    elif t == "v":
                        for g in range(2):
                            for n, i0 in ((7, 0), (1, 7)):
                                at = g * 64 + i0 * HD
                                nc.vector.tensor_tensor(every_136(vp, everything, g * 1024 + i0 * 136, n),
                                                        heads(psO[:, 160 + at:160 + at + n * HD]),
                                                        heads(w("v_b", at=at, n=n * HD)), ALU.add)
                        for j in range(4):
                            rows = slice(32 * j, 32 * j + MREM)
                            for r in range(4):
                                o, at = r * 128 + (r % 2) * 32 + j * HD, (4 * r + j) * HD
                                v0 = cols["v_b"][0] + at
                                last = nc.vector.tensor_tensor(vr[rows, o:o + HD], psO[rows, 288 + at:288 + at + HD],
                                                               W[rows, v0:v0 + HD], ALU.add)
                        last.then_inc(v_done, 1)
                    elif t == "q":
                        dve.wait_ge(q_mm, nth(b))
                        nc.vector.tensor_scalar(qf[:, :], psM[:, :], w("q_b"), SCALE, ALU.add, ALU.mult).then_inc(qf_done, 1)
                    elif t == "mx":
                        tile, g = divmod(i, MX_GROUPS)
                        n = min(3, HEADS - 3 * g)
                        dve.wait_ge(sc_mm, nth(b, i, N_MX))
                        nc.vector.tensor_reduce(mx[:, tile, 3 * g:3 * g + n],
                                                psS[i % 2][:, 0:n * MC].rearrange("p (h m) -> p h m", m=MC),
                                                AX.X, ALU.max).then_inc(mx_done, 1)
                    elif t == "mt":
                        dve.wait_ge(mt_mm, nth(b, NT - 1, NT))
                        nc.vector.tensor_scalar(nmf, psM[0:HEADS, :], -1.0, None, ALU.mult).then_inc(nmf_done, 1)
                    elif t == "o":
                        dve.wait_ge(rden_done, nth(b, i, 2))
                        nc.vector.tensor_tensor(oT[64 * i:64 * i + 64, :], psH[i][0:64, :], rden[:, i, :],
                                                ALU.mult).then_inc(o_done, 1)
                    elif t == "s2":
                        dve.wait_ge(pj_mm, nth(b))
                        nc.vector.scalar_tensor_tensor(out=lnin[1][:, :], in0=psM[:, :], scalar=w("p_b"), in1=x1[:, :],
                                                       op0=ALU.add, op1=ALU.add).then_inc(s2_done, 1)
                    elif t == "logits":
                        dve.wait_ge(r_mm, nth(c, NT - 1, NT))
                        logits = psX[:, 0:NT * E].rearrange("p (c e) -> p c e", e=E)
                        nc.vector.tensor_reduce(lmx[:, :], logits, AX.X, ALU.max).then_inc(lmx_done, 1)
                        dve.wait_ge(lmx_done, nth(c))
                        nc.vector.tensor_tensor(lg[:, :, :], logits, per_tile(lmx[:, :]), ALU.subtract).then_inc(lg_done, 1)
                    elif t == "router":
                        dve.wait_ge(re_done, nth(c))
                        nc.vector.tensor_reduce(psm[:, :], pe_[:, :, :], AX.X, ALU.add)
                        for tile in range(NT):
                            last = nc.vector.max(m8[:, tile, :], pe_[:, tile, :])
                        last.then_inc(max_done, 1)
                        dve.wait_ge(max_done, nth(c))
                        nc.vector.reciprocal(prs[:, :], psm[:, :])
                        for tile in range(NT):
                            last = nc.vector.max_index(ix[:, tile, :], m8[:, tile, :], pe_[:, tile, :])
                        last.then_inc(ix_done, 1)
                        dve.wait_ge(ix_done, nth(c))
                        nc.vector.tensor_copy(ixf[:, :, :], ix[:, :, :]).then_inc(ixf_done, 1)
                        dve.wait_ge(ixf_done, nth(c))
                        iota = w("iota").rearrange("p (c e) -> p c e", e=E)
                        for k in range(2):
                            last = nc.vector.tensor_tensor(mk[:, k, :, :], iota, ixf[:, :, k:k + 1].to_broadcast([128, NT, E]),
                                                           ALU.is_equal)
                        last.then_inc(mk_done, 1)
                        dve.wait_ge(mk_done, nth(c))
                        nc.vector.tensor_tensor(mks[:, :, :], mk[:, 0, :, :], mk[:, 1, :, :], ALU.add).then_inc(mks_done, 1)
                        dve.wait_ge(mks_done, nth(c))
                        nc.vector.tensor_tensor(wgt[:, :, :], mks[:, :, :], pe_[:, :, :], ALU.mult).then_inc(wgt_done, 1)
                        dve.wait_ge(wgt_done, nth(c))
                        nc.vector.tensor_tensor(wgn[:, :, :], wgt[:, :, :], per_tile(prs[:, :]), ALU.mult).then_inc(wgn_done, 1)
                    elif t == "w_third":
                        dve.wait_ge(w_second, nth(c))
                        nc.vector.tensor_tensor(ws[64:64 + E, :], wr, wr2[:, :], ALU.subtract).then_inc(ws_done, 1)
                    elif t == "gate":
                        dve.wait_ge(g_done, nth(c, i, E))
                        dve.wait_ge(wb_mm, nth(c, i, E))
                        nc.vector.tensor_tensor(gl[:, i % 2, :], gl[:, i % 2, :], psO[:, :], ALU.mult).then_inc(gw_done, 1)
                    elif t == "s3":
                        dve.wait_ge(dn_mm, nth(c, E - 1, E))
                        nc.vector.tensor_tensor(lnin[2][:, :], psM[:, :], x2[:, :], ALU.add).then_inc(s3_done, 1)
                    else:
                        assert False, t

            run_steps(walk, dve.Fori)

        @block.tensor
        def _(pe):
            mm = nc.tensor.matmul
            pe.wait_ge(w1_loaded, 16)
            pe.wait_ge(sel_set, 1)
            pe.wait_ge(consts_set, 3)

            def walk(p, b, c):
                for t, i, batch in step_tasks("pe", p, b, c):
                    if t == "z1":
                        pe.wait_ge(xr_loaded if i else x0_loaded, 16)
                        if i:
                            pe.wait_ge(z_done, nth(i - 1))
                        mm(psM[0:R, :], w("w_dt1"), xall[:, i, :], start=True, stop=True).then_inc(z1_mm, 1)
                    elif t == "z2":
                        pe.wait_ge(z1_done, nth(i))
                        mm(psM[:, :], w("w_dt2", R), z1[:, :], start=True, stop=True).then_inc(z2_mm, 1)
                    elif t == "bc":
                        if i:
                            pe.wait_ge(b_done, sum(1 for s, n, k in PLAN["pe"][:PLAN["pe"].index((0, "bc", i))] if n == "b_bcast"))
                        mm(psB[0:96, :], w("w_in3"), xall[:, i, :], start=True, stop=True).then_inc(bc_mm, 1)
                    elif t == "b_bcast":
                        if i == 0:
                            pe.wait_ge(cur_done, nth(p))
                        if isinstance(p, int) and p == 0:
                            pe.wait_ge(bc_first, sum(1 for s, n, k in PLAN["pe"][:PLAN["pe"].index((1, "b_bcast", i))] if n == "bc"))
                        wait_earlier(pe, b_done, p, i, N, 1)
                        mm(psB[:, :], sel[:, i, :], bcs[:, :], start=True, stop=True).then_inc(b_mm, 1)
                    elif t == "c_bcast":
                        wait_earlier(pe, hc_done, p, i, N, 1)
                        mm(psC[:, :], sel[:, N + i, :], bcs[:, :], start=True, stop=True).then_inc(c_mm, 1)
                    elif t == "y":
                        pe.wait_ge(pair_done, nth(p, i, N // 2))
                        if i == 0:
                            wait_earlier(pe, s1_done, p, 0, 1, 1)
                        mm(psY[:, :], ident, hpair[:, i % 2, :], start=(i == 0), stop=(i == N // 2 - 1)).then_inc(y_mm, 1)
                    elif t == "mean":
                        pe.wait_ge((s1_done, s2_done, s3_done)[i], nth(batch))
                        if i == 0:
                            if isinstance(b, int) and b == 0:
                                pe.wait_ge(z_done, B)
                            else:
                                wait_earlier(pe, s2_done, b, 0, 1, 1)
                        if i == 2 and b is not None:
                            pe.wait_ge(nmf_done, nth(b))
                        bank = psX if i == 1 else psM
                        mm(bank[:, :], mean_w[:, :], lnin[i][:, :], start=True, stop=True).then_inc(mean_mm[i], 1)
                    elif t == "var":
                        pe.wait_ge(sq_done[i], nth(batch))
                        bank = psX if i == 1 else psM
                        mm(bank[:, :], mean_w[:, :], rstd[i][:, :], start=True, stop=True).then_inc(var_mm[i], 1)
                    elif t == "kv":
                        pe.wait_ge(w2_loaded, 16)
                        pe.wait_ge(c_copied, nth(b))
                        mm(psO[:, 0:MC], w("k_w", DC), ccur[:, :], start=True, stop=True)
                        mm(psO[:, 160:288], ccur[:, 0:128], w("v_w", DC), start=True, stop=True)
                        for j in range(4):
                            last = mm(psO[32 * j:32 * j + MREM, 288:416], ccur[:, 128:MC], w("v_w", DC), start=True, stop=True)
                        last.then_inc(v_mm, 1)
                    elif t == "q":
                        pe.wait_ge(ln_done[0], nth(b))
                        mm(psM[:, :], w("q_w"), x1[:, :], start=True, stop=True).then_inc(q_mm, 1)
                    elif t == "mx":
                        tile, g = divmod(i, MX_GROUPS)
                        if i == 0:
                            pe.wait_ge(zeroed, 8)
                            pe.wait_ge(q_stacked, nth(b, 143, 144))
                            pe.wait_ge(k_stacked, nth(b, 143, 144))
                        if i >= 2:
                            pe.wait_ge(mx_done, nth(b, i - 2, N_MX))
                        n = min(3, HEADS - 3 * g)
                        for h in range(n):
                            last = mm(psS[i % 2][:, h * MC:(h + 1) * MC], qs[0:9 * HD, 3 * g + h, tile * 128:(tile + 1) * 128],
                                      ks[0:9 * HD, 3 * g + h, 0:MC], start=True, stop=True)
                        last.then_inc(sc_mm, 1)
                    elif t == "mt":
                        pe.wait_ge(mx_done, nth(b, N_MX - 1, N_MX))
                        if c is not None:
                            pe.wait_ge(s3_done, nth(c))
                        else:
                            pe.wait_ge(qf_done, nth(b))
                        for tile in range(NT):
                            nc.tensor.transpose(psM[0:HEADS, tile * 128:(tile + 1) * 128], mx[:, tile, :], ident).then_inc(mt_mm, 1)
                    elif t == "st":
                        r, s = ST_ITEMS[i]
                        if i == 0:
                            pe.wait_ge(ones_set, 17)
                            pe.wait_ge(m_stacked, nth(b, 47, 48))
                        if i >= 2:
                            pe.wait_ge(p_done, nth(b, i - 2, N_ST))
                        if s == 0:
                            for j in range(4):
                                last = mm(psS[i % 2][32 * j:32 * j + MPAD, :], ks[:, 4 * r + j, 128:128 + MPAD],
                                          qs[:, 4 * r + j, :], start=True, stop=True)
                        else:
                            h = 4 * r + s - 1
                            last = mm(psS[i % 2][:, :], ks[:, h, 0:128], qs[:, h, :], start=True, stop=True)
                        last.then_inc(st_mm, 1)
                    elif t == "pv":
                        r, s = ST_ITEMS[i]
                        g, k = divmod(i, N_ST // 2)
                        if k == 0 and c is not None:
                            pe.wait_ge((gw_done, g_done)[g], nth(c, E - 1, E))
                        if i == 0:
                            pe.wait_ge(v_done, nth(b))
                        pe.wait_ge(p_done, nth(b, i, N_ST))
                        vals = vr[:, r * 128:(r + 1) * 128] if s == 0 else vp[:, (4 * r + s - 1) * 128:(4 * r + s) * 128]
                        mm(psH[g][:, :], vals, pt[:, i % 3, :], start=(k == 0), stop=(k == N_ST // 2 - 1)).then_inc(pv_mm, 1)
                    elif t == "proj":
                        pe.wait_ge(o_done, nth(b, 1, 2))
                        if c is not None:
                            pe.wait_ge(lnv_done[2], nth(c))
                        mm(psM[:, :], w("p_w"), oT[:, :], start=True, stop=True).then_inc(pj_mm, 1)
                    elif t == "logits":
                        pe.wait_ge(ln_done[1], nth(c))
                        for tile in range(NT):
                            mm(psX[:, tile * E:(tile + 1) * E], x2[:, tile * 128:(tile + 1) * 128], w("r_w"),
                               start=True, stop=True).then_inc(r_mm, 1)
                    elif t == "wt":
                        pe.wait_ge(wgn_done, nth(c))
                        for tile in range(NT):
                            nc.tensor.transpose(psX[0:E, tile * 128:(tile + 1) * 128], wgn[:, tile, :], ident).then_inc(wt_mm, 1)
                    elif t == "up":
                        if i == 0:
                            pe.wait_ge(w_first, nth(c))
                            if b is not None:
                                pe.wait_ge(qf_done, nth(b))
                                pe.wait_ge(v_done, nth(b))
                            else:
                                pe.wait_ge(s2_done, B)
                            mm(psM[:, :], w("e_bout", E), wT, start=True, stop=False)
                        else:
                            pe.wait_ge(g_done, nth(c, i - 1, E))
                        mm(psX[:, :], w("e_win", at=i * D, n=D), x2[:, :], start=True, stop=True).then_inc(up_mm, 1)
                        if i == 0:
                            pe.wait_ge(ws_done, nth(c))
                        else:
                            pe.wait_ge(gw_done, nth(c, i - 1, E))
                        mm(psO[:, :], sel[:, i, :], ws[:, :], start=True, stop=True).then_inc(wb_mm, 1)
                    elif t == "down":
                        pe.wait_ge(gw_done, nth(c, i, E))
                        mm(psM[:, :], w("e_wout", at=i * D, n=D), gl[:, i % 2, :], start=False,
                           stop=(i == E - 1)).then_inc(dn_mm, 1)
                    else:
                        assert False, t

            run_steps(walk, pe.Fori)


def kernel(**inputs):
    import numpy as _np
    import concourse.bacc as _bacc
    from concourse import mybir as _mybir
    from concourse.bass_utils import run_bass_kernel_spmd as _run

    x = {k: _np.asarray(v) for k, v in inputs.items()}
    cols, width = pack_layout()
    pack = _np.zeros((128, width), _np.float32)

    def put(name, a):
        first, n = cols[name]
        pack[0:a.shape[0], first:first + n] = a

    dh = _np.arange(D).reshape(HEADS, HD).T.reshape(-1)
    kv_w, kv_b = x["L0_xattn_kv_w"], x["L0_xattn_kv_b"]
    put("w_in3", _np.tile(x["L0_attn_W_in"], (1, 3)))
    put("w_dt1", x["L0_attn_W_dt1"])
    put("w_dt2", x["L0_attn_W_dt2"])
    put("A", x["L0_attn_A"].reshape(D, N))
    put("D", x["L0_attn_D"].reshape(D, 1))
    put("b_dt2", x["L0_attn_b_dt2"].reshape(D, 1))
    put("b_dt1", x["L0_attn_b_dt1"].reshape(R, 1))
    put("b_in3", _np.tile(x["L0_attn_b_in"], 3).reshape(96, 1))
    put("eye3", _np.tile(_np.eye(32, dtype=_np.float32), (3, 1)))
    put("ident", _np.eye(128, dtype=_np.float32))
    put("iota", _np.tile(_np.arange(E, dtype=_np.float32), (128, NT)))
    put("q_w", x["L0_xattn_q_w"][:, dh])
    put("q_b", x["L0_xattn_q_b"][dh].reshape(D, 1))
    put("k_w", kv_w[:, 0:D][:, dh])
    put("k_b", kv_b[0:D][dh].reshape(D, 1))
    put("v_w", kv_w[:, D:2 * D])
    put("v_b", _np.tile(kv_b[D:2 * D].reshape(1, D), (128, 1)))
    put("p_w", x["L0_xattn_proj_w"])
    put("p_b", x["L0_xattn_proj_b"].reshape(D, 1))
    put("r_w", x["L0_ffn_router_w"])
    put("e_bin", x["L0_ffn_b_in"].T)
    put("e_bout", x["L0_ffn_b_out"])
    put("e_win", x["L0_ffn_w_in"].transpose(1, 0, 2).reshape(D, E * D))
    put("e_wout", x["L0_ffn_w_out"].transpose(1, 0, 2).reshape(D, E * D))
    arrays = {
        "in_xT": _np.ascontiguousarray(x["x"].transpose(2, 0, 1)),
        "in_ctxT": _np.ascontiguousarray(x["ctx_768"].transpose(2, 0, 1)),
        "in_pack": pack,
    }
    nc = _bacc.Bacc("TRN2", target_bir_lowering=False, num_devices=1)
    args = [nc.dram_tensor(n, a.shape, _mybir.dt.from_np(a.dtype), kind="ExternalInput").ap() for n, a in arrays.items()]
    args.append(nc.dram_tensor("out_T", (B, D, L), _mybir.dt.float32, kind="ExternalOutput").ap())
    decoder_block(nc, *args)
    r = _run(nc, [arrays], core_ids=[0])
    return _np.ascontiguousarray(r.results[0]["out_T"].transpose(0, 2, 1))
```

```python
import concourse.bass as bass
from concourse import mybir
from contextlib import ExitStack

B, L, D, N, R = 4, 512, 128, 16, 64
HEADS, HD = 16, 8
MC, DC = 154, 96
MREM = MC - 128
MPAD = 32
E, NT = 8, L // 128
DT_MIN, DT_MAX, EPS = 1e-7, 1e6, 1e-5
SCALE = float(HD) ** -0.5
MAXROW = 96
KS = MAXROW + 3


def pack_layout():
    widths = [("w_in", 2 * N), ("w_dt1", R), ("w_dt2", D), ("A", N), ("D", 1), ("b_dt2", 1), ("b_dt1", 1),
              ("b_in", 1), ("eye3", E), ("ident", 128), ("centre", 128), ("iota", NT * E),
              ("q_w", D), ("q_b", 1), ("k_w", D), ("k_b", 1), ("v_w", D), ("v_b", D), ("p_w", D), ("p_b", 1),
              ("r_w", E), ("e_bin", E), ("e_bout", D), ("e_win", E * D), ("e_wout", E * D)]
    at, out = 0, {}
    for name, w in widths:
        out[name] = (at, w)
        at += w
    return out, at


ST_ITEMS = [(r, s) for r in range(4) for s in range(5)]
N_ST = len(ST_ITEMS)
N_BC = 4
N_ABAR = 8
N_GL = 3
MX_GROUPS = -(-HEADS // 3)
HH = HEADS // 2
MX_ITEMS = [(tile, 3 * g, min(3 * g + 3, HEADS)) for g in range(3) for tile in range(NT)] + [None] + \
    [(tile, 3 * g, min(3 * g + 3, HEADS)) for g in range(3, MX_GROUPS) for tile in range(NT)] + [None]
N_MX = len(MX_ITEMS)


STEP = 66
DT_AT, DT_LAG = (-36, 10, 23, 51), 15.8
SCAN_AT = (3, 8.0, 16, 22, 27, 31.7, 34.5, 37, 39.3, 41.5, 43.8, 46, 48.3, 50.2, 52.7, 55.2)
U_LAG, PAIR_LAG, Y_LAG = -1.3, 2.5, 4.3
ABAR_AT, ABAR_LAG = 2.6, 0.6
S1_AT = 59.8
LN0_AT, K_AT, Q_AT, V_AT, RES_AT = 61.3, 47, 67.2, 11.5, 6.7
MX_AT, MX_STEP, MX1_AT, MX1_STEP = 13, 0.87, 27, 0.9
ST_AT, ST1_AT, ST_STEP, PV_LAG, O_LAG = 31, 46.0, 1.453, 1.6, 0.5
M_ENGINE = 'pool'
ROUTER_AT = 8
UP_AT, UP_LAG = (8.3, 10.3, 12), -3.8
GATE_AT = (14.8, 17.0, 18.9, 21.1, 23.3, 25.5, 27.7, 29.9)
DOWN_LAG, LN2_LAG = 2.0, 7.6


def plan():
    tasks = []

    def add(stage, at, engine, name, i=0):
        if stage == 1 and at >= STEP:
            stage, at = 2, at - STEP
        tasks.append((at, len(tasks), engine, stage, name, i))

    for q, at in enumerate(DT_AT):
        for d, engine, name in (
                (0, "pe", "bc"), (0.5, "act", "bc"), (1, "sp", "bc"), (0.6, "pe", "z1"), (1, "act", "z1"), (2, "pe", "z2"),
                (3, "act", "z"), (4, "act", "softplus"), (DT_LAG, "dve", "dt")):
            add(0, at + d, engine, name, q)

    add(1, -3, "dve", "cur")
    for n, t in enumerate(SCAN_AT):
        ahead = SCAN_AT[n - 2] if n >= 2 else -2 + 2 * n
        if n % 2 == 0:
            add(1, SCAN_AT[n - 8] + 5 if n >= 8 else -4 + 0.1 * n, "sp", "bcast", n // 2)
        add(1, ahead + U_LAG, "pool", "u", n)
        add(1, (-1 if n == 0 else ABAR_AT + ABAR_LAG * n) if n < 8 else max(ahead, ST_AT - 0.5), "act", "a_bar", n)
        add(1, t - 0.1 if n == 0 else max(SCAN_AT[n - 1] + 0.1, ST_AT) if n >= 8 else SCAN_AT[n - 1] + 0.1, "dve", "bbar", n)
        add(1, t, "dve", "scan", n)
        add(1, t + 0.2, "dve", "hc", n)
        if n % 2:
            add(1, t + PAIR_LAG, "pool", "pair", n // 2)
        if n % 4 == 3:
            add(1, t + Y_LAG, "pe", "y", n // 4)
    add(1, S1_AT, "dve", "s1")

    def norm(stage, k, at):
        for d, engine, name in ((0, "pe", "centre"), (1, "act", "square"), (1.7, "pe", "var"),
                                (2.7, "act", "rstd"), (4.2, "dve", "norm")):
            add(stage, at + d, engine, name, k)

    def parts(stage, at, what, subtract):
        for d, engine, name in ((0, "act", "first"), (0.7, subtract, "rest"), (1.7, "act", "second"), (2.4, subtract, "third")):
            add(stage, at + d, engine, name, what)

    add(1, K_AT - 4, "pool", "ctx")
    add(1, K_AT, "pe", "k")
    add(1, K_AT + 0.5, "dve", "k")
    parts(1, K_AT + 1, "k", "pool")
    norm(1, 0, LN0_AT)
    add(1, Q_AT, "pe", "q")
    add(1, Q_AT + 1, "dve", "q")
    parts(1, Q_AT + 1.6, "q", "pool")

    add(1, K_AT + 5, "sp", "k_store")
    for j in range(3):
        add(2, Q_AT - STEP + 2.5 + j, "sp", "q_store", j)
    add(2, Q_AT - STEP + 1, "sp", "k_stack")
    for j in range(3):
        add(2, Q_AT - STEP + (4.5, 5.5, 6.5)[j], "sp", "q_stack", j)
    add(2, V_AT - 2, "pe", "v")
    add(2, V_AT, "dve", "v")
    add(2, RES_AT, "act", "res")
    for k, item in enumerate(MX_ITEMS):
        half = k // (N_MX // 2)
        at = (MX_AT + MX_STEP * k, MX1_AT + MX1_STEP * (k - N_MX // 2))[half]
        if item:
            add(2, at, "pe", "mx", k)
            add(2, at + 0.5, "dve", "mx", k)
        else:
            add(2, at, "pe", "mt", k)
            add(2, at + 0.5, "dve", "mt", k)
            parts(2, at + 1, f"m{half}", M_ENGINE)
            for j, name in enumerate(("first", "second", "third")):
                add(2, at + (1.8, 3.6, 4.5)[j], "sp", name, f"m{half}")
    for j in range(N_ST):
        at = ST_AT + ST_STEP * j if j < N_ST // 2 else ST1_AT + ST_STEP * (j - N_ST // 2)
        add(2, at, "pe", "st", j)
        add(2, at + 0.5, "act", "p", j)
        add(2, at + PV_LAG, "pe", "pv", j)
    end = ST1_AT + ST_STEP * N_ST // 2 + 2
    for g, at in ((0, ST_AT + ST_STEP * 10 + 1.5 + O_LAG), (1, end)):
        add(2, at, "act", "rden", g)
        add(2, at + 1, "dve", "o", g)
    add(2, end + 1.5, "pe", "proj")
    add(2, end + 2.5, "dve", "s2")

    norm(3, 1, 0)
    for d, engine, name in ((-1.3, "pe", "logits"), (-0.8, "dve", "logits"), (-0.5, "act", "router_exp"), (0, "dve", "router"),
                            (3.2, "pe", "wt"), (3.7, "act", "w_first"), (4.4, "dve", "w_rest"), (5.7, "act", "w_second"),
                            (6.3, "dve", "w_third"), (0.5, "act", "gelu_table")):
        add(3, ROUTER_AT + d, engine, name)
    for e, gate in enumerate(GATE_AT):
        up = UP_AT[e] if e < 3 else gate + UP_LAG
        add(3, up, "pe", "up", e)
        add(3, up + 0.8, "act", "gelu", e)
        add(3, gate - 0.4, "pe", "gate", e)
        add(3, gate, "dve", "gate", e)
        add(3, gate + DOWN_LAG, "pe", "down", e)
    end = GATE_AT[-1]
    add(3, end + 1.6, "dve", "s3")
    add(3, end, "act", "exp_table")
    norm(3, 2, end + LN2_LAG)
    add(3, end + LN2_LAG + 5, "sp", "out")
    tasks.sort()
    return {e: [(stage, name, i) for _, _, f, stage, name, i in tasks if f == e] for e in ("pe", "act", "dve", "pool", "sp")}


PLAN = plan()


def decoder_block(nc, xT, ctxT, wpack, bc_dram, k_dram, q_dram, out):
    F32, BF16, U32 = mybir.dt.float32, mybir.dt.bfloat16, mybir.dt.uint32
    ALU, ACT, AX = mybir.AluOpType, mybir.ActivationFunctionType, mybir.AxisListType
    cols, WC = pack_layout()
    ctx = ExitStack()
    with ctx:
        def sb(name, shape, dt=F32):
            return ctx.enter_context(nc.sbuf_tensor(name, shape, dt))

        def sem(name):
            return ctx.enter_context(nc.semaphore(name))

        W = sb("W", [128, WC])
        xall = sb("xall", [128, B, L])
        call = sb("call", [DC, B, MC])
        consts = sb("consts", [128, 2])
        sel = sb("sel", [96, E, 128], BF16)
        mean_w = sb("mean_w", [128, 128])
        onepD = sb("onepD", [128, 1])
        rA = sb("rA", [128, N])
        dtall = sb("dtall", [128, B, L])
        bcb = sb("bcb", [128, N_BC, 4, L])
        xcur = sb("xcur", [128, L])
        z1 = sb("z1", [R, L])
        z = sb("z", [128, L])
        zlog = sb("zlog", [128, L])
        dt = sb("dt", [128, L])
        bcf = sb("bcf", [2 * N, 2, L])
        abar = sb("abar", [128, N_ABAR, L])
        ub = sb("ub", [128, 4, L])
        bbar = sb("bbar", [128, 2, L])
        hst = sb("hst", [128, 2, L])
        hc = sb("hc", [128, 4, L])
        hpair = sb("hpair", [128, 2, L])
        lnin = [sb(f"s{k + 1}", [128, L]) for k in range(3)]
        x1, x2 = sb("x1", [128, L]), sb("x2", [128, L])
        x3 = dtall
        res = sb("res", [128, L])
        rstd = [sb(f"rstd{k + 1}", [128, L]) for k in range(3)]
        ccur = sb("ccur", [DC, MC])
        kf = sb("kf", [128, MC])
        kr = sb("kr", [128, MC])
        kpall = sb("kpall", [128, 3, 128 + MPAD], BF16)
        kp = [kpall[:, j, :] for j in range(3)]
        qf = sb("qf", [128, L])
        qr = zlog
        qp = [sb(f"qp{j}", [128, L], BF16) for j in range(3)]
        ks = sb("ks", [KS, HEADS, 128 + MPAD], BF16)
        qs = sb("qs", [KS, HEADS, L], BF16)
        vp = sb("vp", [128, HEADS * 128 + 64])
        vr = sb("vr", [128, 4 * 128 + 64])
        mx = sb("mx", [128, NT, HEADS])
        nmf = bcf[0:HH, 1, :]
        nmr = bcf[0:HH, 0, :]
        nmp = [sb(f"nmp{j}", [HH, L], BF16) for j in range(3)]
        pt = sb("pt", [128, 3, L])
        rden = sb("rden", [64, 2, L])
        oT = sb("oT", [128, L])
        lmx = sb("lmx", [128, NT])
        lg = sb("lg", [128, NT, E])
        pe_ = sb("pe_", [128, NT, E])
        psm = sb("psm", [128, NT])
        prs = sb("prs", [128, NT])
        m8 = sb("m8", [128, NT, 8])
        ix = sb("ix", [128, NT, 8], U32)
        ixf = sb("ixf", [128, NT, 8])
        mk = sb("mk", [128, 2, NT, E])
        mks = sb("mks", [128, NT, E])
        wgt = sb("wgt", [128, NT, E])
        wgn = sb("wgn", [128, NT, E])
        wT = z1[0:E, :]
        wr = z[0:E, :]
        wr2 = sb("wr2", [E, L], BF16)
        ws = sb("ws", [96, L], BF16)
        gl = sb("gl", [128, N_GL, L])

        def ps(name):
            return ctx.enter_context(nc.psum_tensor(name, [128, 512], F32))

        psY, psS0, psS1, psS2, psH0, psG, psU, psM = [ps(n) for n in ("psY", "psS0", "psS1", "psS2", "psH0", "psG", "psU", "psM")]
        psS, psH = [psS0, psS1, psS2], [psH0, psU]
        psXc, psVar = [psS0, psU, psM], [psS1, psG, psG]

        def w(name, rows=128, at=0, n=None):
            first, width = cols[name]
            return W[0:rows, first + at:first + at + (width if n is None else n)]

        ident = w("ident")

        def sems(names):
            return [sem(n) for n in names.split()]

        w0_loaded, w1_loaded, w2_loaded, x0_loaded, xr_loaded, c_loaded, stored = sems(
            "w0_loaded w1_loaded w2_loaded x0_loaded xr_loaded c_loaded stored")
        consts_set, sel_set, inv_done, zeroed, parts_zeroed, q_zeroed, ones_set = sems(
            "consts_set sel_set inv_done zeroed parts_zeroed q_zeroed ones_set")
        z1_mm, z1_done, z2_mm, z_done, zabs_done, zexp_done, zlog_done, dtr_done, dt_done = sems(
            "z1_mm z1_done z2_mm z_done zabs_done zexp_done zlog_done dtr_done dt_done")
        bc_mm, bcf_done = sems("bc_mm bcf_done")
        bc_stored = [sem(f"bc_stored{q}") for q in range(B)]
        cur_done, s1_done, pair_done, quad_done, y_mm = sems("cur_done s1_done pair_done quad_done y_mm")
        bc_landed = [sem(f"bc_landed{k}") for k in range(N_BC)]
        a_done, u_done, bb_done, h_done, hc_done = sems("a_done u_done bb_done h_done hc_done")
        centre_mm, sq_done, var_mm, lnv_done, rstd_done, ln_done = [
            [sem(f"{n}{k}") for k in range(3)] for n in "centre_mm sq_done var_mm lnv_done rstd_done ln_done".split()]
        c_copied, v_mm, k_mm, res_done, kf_done, v_done, q_mm, qf_done = sems("c_copied v_mm k_mm res_done kf_done v_done q_mm qf_done")
        first, rest, second, third = [{w_: sem(f"{n}_{w_}") for w_ in "kqm"} for n in ("first", "rest", "second", "third")]
        for d in (first, rest, second, third):
            d["m0"] = d["m1"] = d["m"]
        k_stored, k_stacked, q_stacked, m_stacked = sems("k_stored k_stacked q_stacked m_stacked")
        q_stored = [sem(f"q_stored{j}") for j in range(3)]
        sc_mm, mx_done, mt_mm, nmf_done = sems("sc_mm mx_done mt_mm nmf_done")
        st_mm, p_done, pv_mm, lden_done, rden_done, o_done, pj_mm, s2_done = sems(
            "st_mm p_done pv_mm lden_done rden_done o_done pj_mm s2_done")
        r_mm, lmx_done, lg_done, re_done, max_done, ix_done, ixf_done, mk_done, mks_done, wgt_done, wgn_done = sems(
            "r_mm lmx_done lg_done re_done max_done ix_done ixf_done mk_done mks_done wgt_done wgn_done")
        wt_mm, w_first, w_rest, w_second, ws_done = sems("wt_mm w_first w_rest w_second ws_done")
        up_mm, wb_mm, g_done, gw_done, dn_mm, s3_done = sems("up_mm wb_mm g_done gw_done dn_mm s3_done")

        def nth(batch, i=0, per_batch=1):
            return batch * per_batch + i + 1

        def nth_part(batch, what):
            return nth(batch, int(what[1]), 2) if what[0] == "m" else nth(batch)

        def wait_earlier(eng, what, batch, i, per_batch, lag):
            value = batch * per_batch + i + 1 - lag
            if not isinstance(batch, int) or value > 0:
                eng.wait_ge(what, value)

        def landed(p, k):
            return 16 * (p * (N // 2 // N_BC) + k // N_BC + 1)

        def run_steps(walk, fori):
            walk(0, None, None)
            walk(1, 0, None)
            with fori(0, B - 2) as c:
                walk(c + 2, c + 1, c)
            walk(None, B - 1, B - 2)
            walk(None, None, B - 1)

        def step_tasks(engine, p, b, c):
            batch = {0: p if isinstance(p, int) and p == 0 else None, 1: p, 2: b, 3: c, 4: None}
            return [(name, i, batch[stage], batch[stage + 1]) for stage, name, i in PLAN[engine] if batch[stage] is not None]

        block = ctx.enter_context(nc.Block())

        @block.sync
        def _(sp):
            first_cols, split = cols["eye3"][0], cols["q_w"][0]
            sp.dma_start(W[:, 0:first_cols], wpack[:, 0:first_cols]).then_inc(w0_loaded, 16)
            sp.dma_start(xall[:, 0, :], xT[:, 0, :]).then_inc(x0_loaded, 16)
            sp.dma_start(W[:, first_cols:split], wpack[:, first_cols:split]).then_inc(w1_loaded, 16)
            sp.dma_start(xall[:, 1:B, :], xT[:, 1:B, :]).then_inc(xr_loaded, 16)
            sp.dma_start(call[:, :, :], ctxT).then_inc(c_loaded, 16)
            sp.dma_start(W[:, split:WC], wpack[:, split:WC]).then_inc(w2_loaded, 16)
            parts_of = {"first": first, "second": second, "third": third}

            def walk(p, b, c):
                for t, i, batch, before in step_tasks("sp", p, b, c):
                    if t == "bc":
                        sp.wait_ge(bcf_done, nth(i))
                        sp.dma_start(bc_dram[i, :, :].rearrange("k (r t) -> (k r) t", t=L), bcf[:, i % 2, :]).then_inc(bc_stored[i], 16)
                    elif t == "bcast":
                        if isinstance(p, int) and i == 0:
                            sp.wait_ge(bc_stored[p], 16)
                        wait_earlier(sp, hc_done, p, 2 * i + 1, N, 2 * N_BC)
                        sp.dma_start(bcb[:, i % N_BC, :, :].rearrange("q r t -> q (r t)"),
                                     bc_dram[bass.ds(p, 1), i, :].to_broadcast([128, 4 * L])).then_inc(bc_landed[i % N_BC], 16)
                    elif t == "out":
                        sp.wait_ge(ln_done[2], nth(c))
                        sp.dma_start(out[bass.ds(c, 1), :, :], x3[:, bass.ds(c, 1), :]).then_inc(stored, 16)
                    elif t == "k_stack":
                        if isinstance(b, int) and b == 0 and i == 0:
                            sp.wait_ge(ones_set, 17)
                            sp.wait_ge(q_zeroed, 1)
                        sp.wait_ge(k_stored, nth(b, 15, 16))
                        if c is not None:
                            sp.wait_ge(st_mm, nth(c, N_ST - 1, N_ST))
                        sp.dma_start(ks[0:9 * HD, :, :].rearrange("r h m -> r (h m)"),
                                     k_dram[bass.ds(b, 1), :, :].rearrange("o (r h) m -> o r (h m)", h=HEADS).partition_broadcast(3)).then_inc(k_stacked, 16)
                    elif t == "k_store":
                        sp.wait_ge(third["k"], nth(p))
                        sp.dma_start(k_dram[bass.ds(p, 1), :, :].rearrange("o (j q) m -> q (o j) m", j=3), kpall[:, :, :]).then_inc(k_stored, 16)
                    elif t == "q_store":
                        sp.wait_ge((first, second, third)[i]["q"], nth(b))
                        sp.dma_start(q_dram[bass.ds(b, 1), i, :, :], qp[i][:, :]).then_inc(q_stored[i], 16)
                    elif t == "q_stack":
                        sp.wait_ge(q_stored[i], nth(b, 15, 16))
                        src = q_dram[bass.ds(b, 1), i, :, :].rearrange("o (d h) t -> o d (h t)", h=HEADS)
                        rows = slice(i * 3 * HD, (i + 1) * 3 * HD)
                        sp.dma_start(qs[rows, :, :].rearrange("r h t -> r (h t)"), src.partition_broadcast(3)).then_inc(q_stacked, 16)
                    elif i in ("m0", "m1"):
                        j, half = ("first", "second", "third").index(t), int(i[1])
                        sp.wait_ge(parts_of[t]["m"], nth(b, half, 2))
                        sp.dma_start(qs[MAXROW + j:MAXROW + j + 1, half * HH:(half + 1) * HH, :], nmp[j][:, :]).then_inc(m_stacked, 16)
                    else:
                        assert False, t

            run_steps(walk, sp.Fori)
            sp.wait_ge(stored, 16 * B)

        @block.gpsimd
        def _(pool):
            pool.memset(consts[:, 0:1], EPS).then_inc(consts_set, 1)
            pool.memset(consts[:, 1:2], 1.0).then_inc(consts_set, 1)
            pool.memset(mean_w[:, :], 1.0 / D).then_inc(consts_set, 1)
            pool.memset(kpall[:, :, :].bitcast(U32), 0).then_inc(parts_zeroed, 1)
            pool.memset(ws[:, :].bitcast(U32), 0).then_inc(parts_zeroed, 1)
            pool.wait_ge(parts_zeroed, 2)
            pool.memset(qs[64:96, :, :].rearrange("p h m -> p (h m)").bitcast(U32), 0).then_inc(q_zeroed, 1)
            pool.wait_ge(q_zeroed, 1)
            pool.wait_ge(w1_loaded, 16)
            pool.tensor_copy(sel[:, :, :], w("eye3", 96).unsqueeze(2).to_broadcast([96, E, 128])).then_inc(sel_set, 1)

            whole_of = {"k": (kf[:, :], kr[:, :], [t[:, 0:MC] for t in kp], kf_done),
                        "q": (qf[:, :], qr[:, :], [t[:, :] for t in qp], qf_done),
                        "m0": (nmf, nmr, [t[:, :] for t in nmp], nmf_done), "m1": (nmf, nmr, [t[:, :] for t in nmp], nmf_done)}

            def walk(p, b, c):
                for t, i, batch, before in step_tasks("pool", p, b, c):
                    if t == "u":
                        if i == 0:
                            pool.wait_ge(cur_done, nth(p))
                        wait_earlier(pool, bb_done, p, i, N, 4)
                        k, r = divmod(i, 2)
                        pool.wait_ge(bc_landed[k % N_BC], landed(p, k))
                        pool.tensor_tensor(ub[:, i % 4, :], bcb[:, k % N_BC, r, :], xcur[:, :], ALU.mult).then_inc(u_done, 1)
                    elif t == "pair":
                        pool.wait_ge(hc_done, nth(p, 2 * i + 1, N))
                        if i % 2 == 0:
                            wait_earlier(pool, y_mm, p, i // 2, N // 4, 1)
                        pool.tensor_tensor(hpair[:, i % 2, :], hc[:, 2 * i % 4, :], hc[:, (2 * i + 1) % 4, :],
                                           ALU.add).then_inc(pair_done, 1)
                        if i % 2:
                            pool.wait_ge(pair_done, nth(p, i, N // 2))
                            pool.tensor_tensor(hpair[:, 0, :], hpair[:, 0, :], hpair[:, 1, :], ALU.add).then_inc(quad_done, 1)
                    elif t == "ctx":
                        pool.wait_ge(c_loaded, 16)
                        if b is not None:
                            pool.wait_ge(v_mm, nth(b))
                        pool.tensor_copy(ccur[:, :], call[:, bass.ds(p, 1), :]).then_inc(c_copied, 1)
                    elif t == "rest":
                        whole, left, parts, whole_done = whole_of[i]
                        pool.wait_ge(first[i], nth_part(batch, i))
                        pool.tensor_tensor(left, whole, parts[0], ALU.subtract).then_inc(rest[i], 1)
                    elif t == "third":
                        whole, left, parts, whole_done = whole_of[i]
                        pool.wait_ge(second[i], nth_part(batch, i))
                        pool.tensor_tensor(parts[2], left, parts[1], ALU.subtract).then_inc(third[i], 1)
                    else:
                        assert False, t

            run_steps(walk, pool.Fori)

        @block.scalar
        def _(act):
            eps, one = consts[:, 0:1], consts[:, 1:2]
            whole_of = {"k": (kf[:, :], kr[:, :], [t[:, 0:MC] for t in kp], kf_done),
                        "q": (qf[:, :], qr[:, :], [t[:, :] for t in qp], qf_done),
                        "m0": (nmf, nmr, [t[:, :] for t in nmp], nmf_done), "m1": (nmf, nmr, [t[:, :] for t in nmp], nmf_done)}
            nc.scalar.preload_act_table_set("natural_log_exp_and_others")
            act.wait_ge(w0_loaded, 16)
            act.wait_ge(consts_set, 3)

            def walk(p, b, c):
                if p is None or not isinstance(p, int) or p:
                    nc.scalar.preload_act_table_set("natural_log_exp_and_others")
                for t, i, batch, before in step_tasks("act", p, b, c):
                    if t == "z1":
                        act.wait_ge(z1_mm, nth(i))
                        nc.scalar.activation(z1[:, :], psM[0:R, :], ACT.Identity, bias=w("b_dt1", R)).then_inc(z1_done, 1)
                    elif t == "z":
                        act.wait_ge(z2_mm, nth(i))
                        wait_earlier(act, dtr_done, i, 0, 1, 1)
                        nc.scalar.activation(z[:, :], psM[:, :], ACT.Identity, bias=w("b_dt2")).then_inc(z_done, 1)
                    elif t == "softplus":
                        act.wait_ge(z_done, nth(i))
                        nc.scalar.activation(zlog[:, :], z[:, :], ACT.Abs).then_inc(zabs_done, 1)
                        act.wait_ge(zabs_done, nth(i))
                        nc.scalar.activation(zlog[:, :], zlog[:, :], ACT.Exp, scale=-1.0).then_inc(zexp_done, 1)
                        act.wait_ge(zexp_done, nth(i))
                        nc.scalar.activation(zlog[:, :], zlog[:, :], ACT.Ln, bias=one).then_inc(zlog_done, 1)
                    elif t == "bc":
                        act.wait_ge(bc_mm, nth(i))
                        if i >= 2:
                            act.wait_ge(bc_stored[i - 2], 16)
                        nc.scalar.activation(bcf[:, i % 2, :], psS2[0:2 * N, :], ACT.Identity, bias=w("b_in", 2 * N)).then_inc(bcf_done, 1)
                    elif t == "a_bar":
                        if i == 0:
                            act.wait_ge(cur_done, nth(p))
                        wait_earlier(act, h_done, p, i, N, N_ABAR)
                        nc.scalar.activation(abar[:, i % N_ABAR, :], dt[:, :], ACT.Exp, scale=w("A", at=i, n=1)).then_inc(a_done, 1)
                    elif t == "square":
                        act.wait_ge(centre_mm[i], nth(batch))
                        nc.scalar.activation(rstd[i][:, :], psXc[i][:, :], ACT.Square).then_inc(sq_done[i], 1)
                    elif t == "rstd":
                        act.wait_ge(var_mm[i], nth(batch))
                        nc.scalar.activation(rstd[i][:, :], psVar[i][:, :], ACT.Ln, bias=eps).then_inc(lnv_done[i], 1)
                        act.wait_ge(lnv_done[i], nth(batch))
                        nc.scalar.activation(rstd[i][:, :], rstd[i][:, :], ACT.Exp, scale=-0.5).then_inc(rstd_done[i], 1)
                    elif t == "first":
                        whole, left, parts, whole_done = whole_of[i]
                        if i == "k":
                            act.wait_ge(parts_zeroed, 2)
                        if i == "m1":
                            act.wait_ge(m_stacked, nth(b, 47, 96))
                        if i in ("k", "q") and before is not None:
                            act.wait_ge(k_stored if i == "k" else q_stored[0], nth(before, 15, 16))
                        act.wait_ge(whole_done, nth_part(batch, i))
                        nc.scalar.copy(parts[0], whole).then_inc(first[i], 1)
                    elif t == "second":
                        whole, left, parts, whole_done = whole_of[i]
                        act.wait_ge(rest[i], nth_part(batch, i))
                        nc.scalar.copy(parts[1], left).then_inc(second[i], 1)
                    elif t == "p":
                        act.wait_ge(st_mm, nth(b, i, N_ST))
                        if i >= 3:
                            act.wait_ge(pv_mm, nth(b, i - 3, N_ST))
                        nc.scalar.activation(pt[:, i % 3, :], psS[2][:, :], ACT.Exp).then_inc(p_done, 1)
                    elif t == "res":
                        act.wait_ge(ln_done[0], nth(b))
                        nc.scalar.activation(res[:, :], x1[:, :], ACT.Identity, bias=w("p_b")).then_inc(res_done, 1)
                    elif t == "rden":
                        act.wait_ge(pv_mm, nth(b, (i + 1) * N_ST // 2 - 1, N_ST))
                        nc.scalar.activation(rden[:, i, :], psH[i][64:128, :], ACT.Ln).then_inc(lden_done, 1)
                        act.wait_ge(lden_done, nth(b, i, 2))
                        nc.scalar.activation(rden[:, i, :], rden[:, i, :], ACT.Exp, scale=-1.0).then_inc(rden_done, 1)
                    elif t == "router_exp":
                        act.wait_ge(lg_done, nth(c))
                        nc.scalar.activation(pe_[:, :, :], lg[:, :, :], ACT.Exp).then_inc(re_done, 1)
                    elif t == "w_first":
                        act.wait_ge(wt_mm, nth(c, NT - 1, NT))
                        nc.scalar.copy(wT, psG[0:E, :])
                        nc.scalar.copy(ws[0:E, :], psG[0:E, :]).then_inc(w_first, 1)
                    elif t == "w_second":
                        act.wait_ge(w_rest, nth(c))
                        nc.scalar.copy(ws[32:32 + E, :], wr)
                        nc.scalar.copy(wr2[:, :], wr).then_inc(w_second, 1)
                    elif t == "gelu_table":
                        nc.scalar.preload_act_table(ACT.Gelu_apprx_tanh)
                    elif t == "exp_table":
                        nc.scalar.preload_act_table_set("natural_log_exp_and_others")
                    elif t == "gelu":
                        act.wait_ge(up_mm, nth(c, i, E))
                        if i >= N_GL:
                            act.wait_ge(dn_mm, nth(c, i - N_GL, E))
                        nc.scalar.activation(gl[:, i % N_GL, :], psU[:, :], ACT.Gelu_apprx_tanh,
                                             bias=w("e_bin", at=i, n=1)).then_inc(g_done, 1)
                    else:
                        assert False, t

            run_steps(walk, act.Fori)

        @block.vector
        def _(dve):
            nc.vector.memset(ks[:, :, :].rearrange("p h m -> p (h m)").bitcast(U32), 0).then_inc(zeroed, 1)
            nc.vector.memset(vr[:, :], 0.0).then_inc(zeroed, 1)
            nc.vector.memset(vp[:, :], 0.0).then_inc(zeroed, 1)
            dve.wait_ge(zeroed, 3)
            nc.vector.memset(ks[MAXROW:KS, :, 0:MC], 1.0).then_inc(ones_set, 1)

            def every_136(tile, rows, at, n):
                if n == 1:
                    return tile[rows, at:at + HD].rearrange("p (h c) -> p h c", c=HD)
                return tile[rows, at:at + n * 136].rearrange("p (h c) -> p h c", c=136)[:, :, 0:HD]

            everything = slice(0, 128)
            for g in range(2):
                for n, i0 in ((7, 0), (1, 7)):
                    nc.vector.memset(every_136(vp, everything, g * 1024 + i0 * 136 + 64, n), 1.0)
            for j in range(4):
                for r in range(4):
                    o = r * 128 + (r % 2) * 32 + j * HD + 64
                    nc.vector.memset(vr[32 * j:32 * j + MREM, o:o + HD], 1.0).then_inc(ones_set, 1)
            dve.wait_ge(w0_loaded, 16)
            nc.vector.reciprocal(rA[:, :], w("A")).then_inc(inv_done, 1)
            nc.vector.tensor_scalar(onepD[:, :], w("D"), 1.0, None, ALU.add).then_inc(inv_done, 1)
            dve.wait_ge(inv_done, 2)

            whole_of = {"k": (kf[:, :], kr[:, :], [t[:, 0:MC] for t in kp], kf_done),
                        "q": (qf[:, :], qr[:, :], [t[:, :] for t in qp], qf_done),
                        "m0": (nmf, nmr, [t[:, :] for t in nmp], nmf_done), "m1": (nmf, nmr, [t[:, :] for t in nmp], nmf_done)}

            def per_tile(ap):
                return ap.unsqueeze(2).to_broadcast([128, NT, E])

            def heads(ap):
                return ap.rearrange("p (h c) -> p h c", c=HD)

            def walk(p, b, c):
                for t, i, batch, before in step_tasks("dve", p, b, c):
                    if t == "dt":
                        dve.wait_ge(zlog_done, nth(i))
                        nc.vector.scalar_tensor_tensor(out=dtall[:, i, :], in0=z[:, :], scalar=0.0, in1=zlog[:, :],
                                                       op0=ALU.max, op1=ALU.add).then_inc(dtr_done, 1)
                        dve.wait_ge(dtr_done, nth(i))
                        nc.vector.tensor_scalar(dtall[:, i, :], dtall[:, i, :], DT_MIN, DT_MAX, ALU.max, ALU.min).then_inc(dt_done, 1)
                    elif t == "cur":
                        if isinstance(p, int):
                            dve.wait_ge(xr_loaded if p else x0_loaded, 16)
                            dve.wait_ge(dt_done, nth(p))
                        wait_earlier(dve, s1_done, p, 0, 1, 1)
                        nc.vector.tensor_copy(dt[:, :], dtall[:, bass.ds(p, 1), :])
                        nc.vector.tensor_copy(xcur[:, :], xall[:, bass.ds(p, 1), :]).then_inc(cur_done, 1)
                    elif t == "bbar":
                        dve.wait_ge(u_done, nth(p, i, N))
                        dve.wait_ge(a_done, nth(p, i, N))
                        nc.vector.scalar_tensor_tensor(out=bbar[:, i % 2, :], in0=abar[:, i % N_ABAR, :], scalar=-1.0, in1=ub[:, i % 4, :],
                                                       op0=ALU.add, op1=ALU.mult).then_inc(bb_done, 1)
                    elif t == "scan":
                        dve.wait_ge(bb_done, nth(p, i, N))
                        nc.vector.tensor_tensor_scan(hst[:, i % 2, :], abar[:, i % N_ABAR, :], bbar[:, i % 2, :], 0.0,
                                                     ALU.mult, ALU.add).then_inc(h_done, 1)
                    elif t == "hc":
                        dve.wait_ge(h_done, nth(p, i, N))
                        k, r = divmod(i, 2)
                        dve.wait_ge(bc_landed[k % N_BC], landed(p, k))
                        wait_earlier(dve, pair_done, p, i // 2, N // 2, 2)
                        nc.vector.scalar_tensor_tensor(out=hc[:, i % 4, :], in0=hst[:, i % 2, :], scalar=rA[:, i:i + 1],
                                                       in1=bcb[:, k % N_BC, 2 + r, :], op0=ALU.mult, op1=ALU.mult).then_inc(hc_done, 1)
                    elif t == "s1":
                        dve.wait_ge(y_mm, nth(p, N // 4 - 1, N // 4))
                        nc.vector.scalar_tensor_tensor(out=lnin[0][:, :], in0=xcur[:, :], scalar=onepD[:, :], in1=psY[:, :],
                                                       op0=ALU.mult, op1=ALU.add).then_inc(s1_done, 1)
                    elif t == "norm":
                        dve.wait_ge(rstd_done[i], nth(batch))
                        if i == 0 and before is not None:
                            dve.wait_ge(res_done, nth(before))
                        dst = (x1[:, :], x2[:, :], x3[:, bass.ds(batch, 1), :])[i]
                        nc.vector.tensor_tensor(dst, psXc[i][:, :], rstd[i][:, :], ALU.mult).then_inc(ln_done[i], 1)
                    elif t == "k":
                        dve.wait_ge(k_mm, nth(batch))
                        nc.vector.tensor_scalar(kf[:, :], psS[1][:, 0:MC], w("k_b"), None, ALU.add).then_inc(kf_done, 1)
                    elif t == "v":
                        dve.wait_ge(v_mm, nth(b))
                        if c is not None:
                            dve.wait_ge(pv_mm, nth(c, N_ST - 1, N_ST))
                        for g in range(2):
                            for n, i0 in ((7, 0), (1, 7)):
                                at = g * 64 + i0 * HD
                                nc.vector.tensor_tensor(every_136(vp, everything, g * 1024 + i0 * 136, n),
                                                        heads(psH[0][:, at:at + n * HD]),
                                                        heads(w("v_b", at=at, n=n * HD)), ALU.add)
                        for j in range(4):
                            rows = slice(32 * j, 32 * j + MREM)
                            for r in range(4):
                                o, at = r * 128 + (r % 2) * 32 + j * HD, (4 * r + j) * HD
                                v0 = cols["v_b"][0] + at
                                last = nc.vector.tensor_tensor(vr[rows, o:o + HD], psH[0][rows, 128 + at:128 + at + HD],
                                                               W[rows, v0:v0 + HD], ALU.add)
                        last.then_inc(v_done, 1)
                    elif t == "q":
                        dve.wait_ge(q_mm, nth(batch))
                        nc.vector.tensor_scalar(qf[:, :], psS[1][:, :], w("q_b"), SCALE, ALU.add, ALU.mult).then_inc(qf_done, 1)
                    elif t == "mx":
                        tile, h0, h1 = MX_ITEMS[i]
                        dve.wait_ge(sc_mm, nth(b, i - i // (N_MX // 2), N_MX - 2))
                        nc.vector.tensor_reduce(mx[:, tile, h0:h1],
                                                psS[i % 2][:, 0:(h1 - h0) * MC].rearrange("p (h m) -> p h m", m=MC),
                                                AX.X, ALU.max).then_inc(mx_done, 1)
                    elif t == "mt":
                        half = i // (N_MX // 2)
                        if half:
                            dve.wait_ge(third["m"], nth(b, 0, 2))
                        dve.wait_ge(mt_mm, nth(b, (half + 1) * NT - 1, 2 * NT))
                        nc.vector.tensor_scalar(nmf, psS[i % 2][0:HH, :], -1.0, None, ALU.mult).then_inc(nmf_done, 1)
                    elif t == "o":
                        dve.wait_ge(rden_done, nth(b, i, 2))
                        nc.vector.tensor_tensor(oT[64 * i:64 * i + 64, :], psH[i][0:64, :], rden[:, i, :],
                                                ALU.mult).then_inc(o_done, 1)
                    elif t == "s2":
                        dve.wait_ge(pj_mm, nth(batch))
                        nc.vector.tensor_tensor(lnin[1][:, :], psH[0][:, :], res[:, :], ALU.add).then_inc(s2_done, 1)
                    elif t == "logits":
                        dve.wait_ge(r_mm, nth(c, NT - 1, NT))
                        logits = psG[:, 0:NT * E].rearrange("p (c e) -> p c e", e=E)
                        nc.vector.tensor_reduce(lmx[:, :], logits, AX.X, ALU.max).then_inc(lmx_done, 1)
                        dve.wait_ge(lmx_done, nth(c))
                        nc.vector.tensor_tensor(lg[:, :, :], logits, per_tile(lmx[:, :]), ALU.subtract).then_inc(lg_done, 1)
                    elif t == "router":
                        dve.wait_ge(re_done, nth(c))
                        nc.vector.tensor_reduce(psm[:, :], pe_[:, :, :], AX.X, ALU.add)
                        for tile in range(NT):
                            last = nc.vector.max(m8[:, tile, :], pe_[:, tile, :])
                        last.then_inc(max_done, 1)
                        dve.wait_ge(max_done, nth(c))
                        nc.vector.reciprocal(prs[:, :], psm[:, :])
                        for tile in range(NT):
                            last = nc.vector.max_index(ix[:, tile, :], m8[:, tile, :], pe_[:, tile, :])
                        last.then_inc(ix_done, 1)
                        dve.wait_ge(ix_done, nth(c))
                        nc.vector.tensor_copy(ixf[:, :, :], ix[:, :, :]).then_inc(ixf_done, 1)
                        dve.wait_ge(ixf_done, nth(c))
                        iota = w("iota").rearrange("p (c e) -> p c e", e=E)
                        for k in range(2):
                            last = nc.vector.tensor_tensor(mk[:, k, :, :], iota, ixf[:, :, k:k + 1].to_broadcast([128, NT, E]),
                                                           ALU.is_equal)
                        last.then_inc(mk_done, 1)
                        dve.wait_ge(mk_done, nth(c))
                        nc.vector.tensor_tensor(mks[:, :, :], mk[:, 0, :, :], mk[:, 1, :, :], ALU.add).then_inc(mks_done, 1)
                        dve.wait_ge(mks_done, nth(c))
                        nc.vector.tensor_tensor(wgt[:, :, :], mks[:, :, :], pe_[:, :, :], ALU.mult).then_inc(wgt_done, 1)
                        dve.wait_ge(wgt_done, nth(c))
                        nc.vector.tensor_tensor(wgn[:, :, :], wgt[:, :, :], per_tile(prs[:, :]), ALU.mult).then_inc(wgn_done, 1)
                    elif t == "rest":
                        whole, left, parts, whole_done = whole_of[i]
                        dve.wait_ge(first[i], nth_part(batch, i))
                        nc.vector.tensor_tensor(left, whole, parts[0], ALU.subtract).then_inc(rest[i], 1)
                    elif t == "third":
                        whole, left, parts, whole_done = whole_of[i]
                        dve.wait_ge(second[i], nth_part(batch, i))
                        nc.vector.tensor_tensor(parts[2], left, parts[1], ALU.subtract).then_inc(third[i], 1)
                    elif t == "w_rest":
                        dve.wait_ge(w_first, nth(c))
                        nc.vector.tensor_tensor(wr, wT, ws[0:E, :], ALU.subtract).then_inc(w_rest, 1)
                    elif t == "w_third":
                        dve.wait_ge(w_second, nth(c))
                        nc.vector.tensor_tensor(ws[64:64 + E, :], wr, wr2[:, :], ALU.subtract).then_inc(ws_done, 1)
                    elif t == "gate":
                        dve.wait_ge(g_done, nth(c, i, E))
                        dve.wait_ge(wb_mm, nth(c, i, E))
                        nc.vector.tensor_tensor(gl[:, i % N_GL, :], gl[:, i % N_GL, :], psG[:, :], ALU.mult).then_inc(gw_done, 1)
                    elif t == "s3":
                        dve.wait_ge(dn_mm, nth(c, E - 1, E))
                        nc.vector.tensor_tensor(lnin[2][:, :], psM[:, :], x2[:, :], ALU.add).then_inc(s3_done, 1)
                    else:
                        assert False, t

            run_steps(walk, dve.Fori)

        @block.tensor
        def _(pe):
            mm = nc.tensor.matmul
            pe.wait_ge(w0_loaded, 16)

            def wait_mx_bank(i, b):
                half = N_MX // 2
                if i >= 2 and MX_ITEMS[i - 2] is None:
                    pe.wait_ge(nmf_done, nth(b, 0, 2))
                elif i >= 2:
                    pe.wait_ge(mx_done, nth(b, i - 2 - (i - 2) // half, N_MX - 2))

            def walk(p, b, c):
                for t, i, batch, before in step_tasks("pe", p, b, c):
                    if t == "z1":
                        pe.wait_ge(xr_loaded if i else x0_loaded, 16)
                        wait_earlier(pe, z_done, i, 0, 1, 1)
                        mm(psM[0:R, :], w("w_dt1"), xall[:, i, :], start=True, stop=True).then_inc(z1_mm, 1)
                    elif t == "z2":
                        pe.wait_ge(z1_done, nth(i))
                        mm(psM[:, :], w("w_dt2", R), z1[:, :], start=True, stop=True).then_inc(z2_mm, 1)
                    elif t == "bc":
                        pe.wait_ge(xr_loaded if i else x0_loaded, 16)
                        wait_earlier(pe, bcf_done, i, 0, 1, 1)
                        mm(psS2[0:2 * N, :], w("w_in"), xall[:, i, :], start=True, stop=True).then_inc(bc_mm, 1)
                    elif t == "y":
                        if isinstance(p, int) and p == 0 and i == 0:
                            pe.wait_ge(w1_loaded, 16)
                            pe.wait_ge(consts_set, 3)
                        pe.wait_ge(quad_done, nth(p, i, N // 4))
                        if i == 0:
                            wait_earlier(pe, s1_done, p, 0, 1, 1)
                        mm(psY[:, :], ident, hpair[:, 0, :], start=(i == 0), stop=(i == N // 4 - 1)).then_inc(y_mm, 1)
                    elif t == "centre":
                        pe.wait_ge((s1_done, s2_done, s3_done)[i], nth(batch))
                        if i == 0 and before is not None:
                            pe.wait_ge(nmf_done, nth(before, 1, 2))
                        mm(psXc[i][:, :], w("centre"), lnin[i][:, :], start=True, stop=True).then_inc(centre_mm[i], 1)
                    elif t == "var":
                        pe.wait_ge(sq_done[i], nth(batch))
                        if i == 0:
                            pe.wait_ge(kf_done, nth(batch))
                        mm(psVar[i][:, :], mean_w[:, :], rstd[i][:, :], start=True, stop=True).then_inc(var_mm[i], 1)
                    elif t == "k":
                        pe.wait_ge(w2_loaded, 16)
                        pe.wait_ge(c_copied, nth(p))
                        if b is not None:
                            pe.wait_ge(nmf_done, nth(b, 1, 2))
                        mm(psS[1][:, 0:MC], w("k_w", DC), ccur[:, :], start=True, stop=True).then_inc(k_mm, 1)
                    elif t == "v":
                        if c is not None:
                            pe.wait_ge(s2_done, nth(c))
                        mm(psH[0][:, 0:128], ccur[:, 0:128], w("v_w", DC), start=True, stop=True)
                        for j in range(4):
                            last = mm(psH[0][32 * j:32 * j + MREM, 128:256], ccur[:, 128:MC], w("v_w", DC), start=True, stop=True)
                        last.then_inc(v_mm, 1)
                    elif t == "q":
                        pe.wait_ge(ln_done[0], nth(batch))
                        mm(psS[1][:, :], w("q_w"), x1[:, :], start=True, stop=True).then_inc(q_mm, 1)
                    elif t == "mx":
                        tile, h0, h1 = MX_ITEMS[i]
                        if i == 0:
                            pe.wait_ge(q_zeroed, 1)
                            pe.wait_ge(q_stacked, nth(b, 47, 48))
                            pe.wait_ge(k_stacked, nth(b, 15, 16))
                            if c is not None:
                                pe.wait_ge(nmf_done, nth(c, 1, 2))
                        wait_mx_bank(i, b)
                        for h in range(h0, h1):
                            last = mm(psS[i % 2][:, (h - h0) * MC:(h - h0 + 1) * MC], qs[0:9 * HD, h, tile * 128:(tile + 1) * 128],
                                      ks[0:9 * HD, h, 0:MC], start=True, stop=True)
                        last.then_inc(sc_mm, 1)
                    elif t == "mt":
                        half = i // (N_MX // 2)
                        pe.wait_ge(mx_done, nth(b, (half + 1) * (N_MX // 2 - 1) - 1, N_MX - 2))
                        for tile in range(NT):
                            nc.tensor.transpose(psS[i % 2][0:HH, tile * 128:(tile + 1) * 128], mx[:, tile, half * HH:(half + 1) * HH],
                                                ident).then_inc(mt_mm, 1)
                    elif t == "st":
                        r, s = ST_ITEMS[i]
                        if i == 0:
                            pe.wait_ge(ones_set, 17)
                            if c is not None:
                                pe.wait_ge(p_done, nth(c, N_ST - 1, N_ST))
                            else:
                                pe.wait_ge(bcf_done, B)
                        if i % (N_ST // 2) == 0:
                            pe.wait_ge(m_stacked, nth(b, 48 * (i // (N_ST // 2)) + 47, 96))
                        if i >= 1:
                            pe.wait_ge(p_done, nth(b, i - 1, N_ST))
                        if s == 0:
                            for j in range(4):
                                last = mm(psS[2][32 * j:32 * j + MPAD, :], ks[:, 4 * r + j, 128:128 + MPAD],
                                          qs[:, 4 * r + j, :], start=True, stop=True)
                        else:
                            h = 4 * r + s - 1
                            last = mm(psS[2][:, :], ks[:, h, 0:128], qs[:, h, :], start=True, stop=True)
                        last.then_inc(st_mm, 1)
                    elif t == "pv":
                        r, s = ST_ITEMS[i]
                        g, k = divmod(i, N_ST // 2)
                        if k == 0 and g and c is not None:
                            pe.wait_ge(g_done, nth(c, E - 1, E))
                        if i == 0:
                            pe.wait_ge(v_done, nth(batch))
                        pe.wait_ge(p_done, nth(b, i, N_ST))
                        vals = vr[:, r * 128:(r + 1) * 128] if s == 0 else vp[:, (4 * r + s - 1) * 128:(4 * r + s) * 128]
                        mm(psH[g][:, :], vals, pt[:, i % 3, :], start=(k == 0), stop=(k == N_ST // 2 - 1)).then_inc(pv_mm, 1)
                    elif t == "proj":
                        pe.wait_ge(o_done, nth(b, 1, 2))
                        mm(psH[0][:, :], w("p_w"), oT[:, :], start=True, stop=True).then_inc(pj_mm, 1)
                    elif t == "logits":
                        pe.wait_ge(ln_done[1], nth(c))
                        for tile in range(NT):
                            mm(psG[:, tile * E:(tile + 1) * E], x2[:, tile * 128:(tile + 1) * 128], w("r_w"),
                               start=True, stop=True).then_inc(r_mm, 1)
                    elif t == "wt":
                        pe.wait_ge(wgn_done, nth(c))
                        for tile in range(NT):
                            nc.tensor.transpose(psG[0:E, tile * 128:(tile + 1) * 128], wgn[:, tile, :], ident).then_inc(wt_mm, 1)
                    elif t == "up":
                        if i == 0:
                            pe.wait_ge(ln_done[1], nth(c))
                        else:
                            pe.wait_ge(g_done, nth(c, i - 1, E))
                        mm(psU[:, :], w("e_win", at=i * D, n=D), x2[:, :], start=True, stop=True).then_inc(up_mm, 1)
                    elif t == "gate":
                        if i == 0:
                            pe.wait_ge(sel_set, 1)
                            pe.wait_ge(w_first, nth(c))
                            mm(psM[:, :], w("e_bout", E), wT, start=True, stop=False)
                            pe.wait_ge(ws_done, nth(c))
                        else:
                            pe.wait_ge(gw_done, nth(c, i - 1, E))
                        mm(psG[:, :], sel[:, i, :], ws[:, :], start=True, stop=True).then_inc(wb_mm, 1)
                    elif t == "down":
                        pe.wait_ge(gw_done, nth(c, i, E))
                        mm(psM[:, :], w("e_wout", at=i * D, n=D), gl[:, i % N_GL, :], start=False,
                           stop=(i == E - 1)).then_inc(dn_mm, 1)
                    else:
                        assert False, t

            run_steps(walk, pe.Fori)


def kernel(**inputs):
    import numpy as _np
    import concourse.bacc as _bacc
    from concourse import mybir as _mybir
    from concourse.bass_utils import run_bass_kernel_spmd as _run

    x = {k: _np.asarray(v) for k, v in inputs.items()}
    cols, width = pack_layout()
    pack = _np.zeros((128, width), _np.float32)

    def put(name, a):
        first, n = cols[name]
        pack[0:a.shape[0], first:first + n] = a

    dh = _np.arange(D).reshape(HEADS, HD).T.reshape(-1)
    kv_w, kv_b = x["L0_xattn_kv_w"], x["L0_xattn_kv_b"]
    bc = _np.arange(2 * N).reshape(2, N // 2, 2).transpose(1, 0, 2).reshape(-1)
    put("w_in", x["L0_attn_W_in"][:, bc])
    put("w_dt1", x["L0_attn_W_dt1"])
    put("w_dt2", x["L0_attn_W_dt2"])
    put("A", x["L0_attn_A"].reshape(D, N))
    put("D", x["L0_attn_D"].reshape(D, 1))
    put("b_dt2", x["L0_attn_b_dt2"].reshape(D, 1))
    put("b_dt1", x["L0_attn_b_dt1"].reshape(R, 1))
    put("b_in", x["L0_attn_b_in"][bc].reshape(2 * N, 1))
    put("eye3", _np.tile(_np.eye(32, dtype=_np.float32)[:, 0:E], (3, 1)))
    put("centre", _np.eye(D, dtype=_np.float32) - _np.float32(1 / D))
    put("ident", _np.eye(128, dtype=_np.float32))
    put("iota", _np.tile(_np.arange(E, dtype=_np.float32), (128, NT)))
    put("q_w", x["L0_xattn_q_w"][:, dh])
    put("q_b", x["L0_xattn_q_b"][dh].reshape(D, 1))
    put("k_w", kv_w[:, 0:D][:, dh])
    put("k_b", kv_b[0:D][dh].reshape(D, 1))
    put("v_w", kv_w[:, D:2 * D])
    put("v_b", _np.tile(kv_b[D:2 * D].reshape(1, D), (128, 1)))
    put("p_w", x["L0_xattn_proj_w"])
    put("p_b", x["L0_xattn_proj_b"].reshape(D, 1))
    put("r_w", x["L0_ffn_router_w"])
    put("e_bin", x["L0_ffn_b_in"].T)
    put("e_bout", x["L0_ffn_b_out"])
    put("e_win", x["L0_ffn_w_in"].transpose(1, 0, 2).reshape(D, E * D))
    put("e_wout", x["L0_ffn_w_out"].transpose(1, 0, 2).reshape(D, E * D))
    arrays = {
        "in_xT": _np.ascontiguousarray(x["x"].transpose(2, 0, 1)),
        "in_ctxT": _np.ascontiguousarray(x["ctx_768"].transpose(2, 0, 1)),
        "in_pack": pack,
    }
    nc = _bacc.Bacc("TRN2", target_bir_lowering=False, num_devices=1)
    args = [nc.dram_tensor(n, a.shape, _mybir.dt.from_np(a.dtype), kind="ExternalInput").ap() for n, a in arrays.items()]
    args.append(nc.dram_tensor("bc_rows", (B, N // 2, 4 * L), _mybir.dt.float32, kind="Internal").ap())
    args.append(nc.dram_tensor("k_parts", (B, 3 * D, 128 + MPAD), _mybir.dt.bfloat16, kind="Internal").ap())
    args.append(nc.dram_tensor("q_parts", (B, 3, D, L), _mybir.dt.bfloat16, kind="Internal").ap())
    args.append(nc.dram_tensor("out_T", (B, D, L), _mybir.dt.float32, kind="ExternalOutput").ap())
    decoder_block(nc, *args)
    r = _run(nc, [arrays], core_ids=[0])
    return _np.ascontiguousarray(r.results[0]["out_T"].transpose(0, 2, 1))
```
